# Optimizing a Trainium2 kernel written in Bass

```python
import numpy as np
import jax
import jax.numpy as jnp

def _softmax(x, axis=-1):
    return jax.nn.softmax(x, axis=axis)

def _gelu(x):
    return jax.nn.gelu(x, approximate=True)

def _silu(x):
    return jax.nn.silu(x)

def _sigmoid(x):
    return jax.nn.sigmoid(x)

def _layernorm(x, axis=-1, eps=1e-05):
    m = jnp.mean(x, axis=axis, keepdims=True)
    v = jnp.var(x, axis=axis, keepdims=True)
    return (x - m) / jnp.sqrt(v + eps)

def _scatter_add(tgt, idx, src, axis=0):
    return tgt.at[idx].add(src)

def _segment_sum(src, seg, n):
    return jax.ops.segment_sum(src, seg, n)
kernel_name = 'mk_seq_preln_d1_jaxref_r8_2ee3ad'

def setup_inputs(seed: int=0):
    np.random.seed(seed)
    _w = jnp.asarray

    def _L0_attn_setup():
        import jax, jax.numpy as jnp
        import numpy as np
        HIDDEN = 256
        KEY = 256
        EPS = 1e-05
        key = jax.random.key(seed)
        k1, k2, k3 = jax.random.split(key, 3)
        B, S = (4, 256)
        x = jax.random.normal(k1, (B, S, HIDDEN), dtype=jnp.float32)
        bq = 1.0 / np.sqrt(HIDDEN)
        qkv = jax.random.uniform(k2, (HIDDEN, KEY * 3), minval=-bq, maxval=bq, dtype=jnp.float32)
        bo = 1.0 / np.sqrt(KEY)
        o_proj = jax.random.uniform(k3, (KEY, HIDDEN), minval=-bo, maxval=bo, dtype=jnp.float32)
        gamma = jnp.ones((HIDDEN,), dtype=jnp.float32)
        beta = jnp.zeros((HIDDEN,), dtype=jnp.float32)
        return {'x': x, 'qkv': qkv, 'o_proj': o_proj, 'gamma': gamma, 'beta': beta}
    _L0_attn_in = _L0_attn_setup()

    def _L0_ffn_setup():
        import jax, jax.numpy as jnp
        import numpy as np
        HIDDEN = 256
        NUM_EXPERTS = 8
        TOP_K = 2
        MOE_INTER = 176
        SHARED_INTER = 704

        def _silu_and_mul(gu):
            i = gu.shape[-1] // 2
            return jax.nn.silu(gu[:, :i]) * gu[:, i:]
        key = jax.random.key(seed)
        ks = jax.random.split(key, 7)
        s = 0.02
        return {'hidden_states': jax.random.normal(ks[0], (2, 256, HIDDEN), dtype=jnp.float32), 'gate_w': jax.random.normal(ks[1], (NUM_EXPERTS, HIDDEN), dtype=jnp.float32) * s, 'shared_gate_w': jax.random.normal(ks[2], (1, HIDDEN), dtype=jnp.float32) * s, 'shared_gate_up_w': jax.random.normal(ks[3], (2 * SHARED_INTER, HIDDEN), dtype=jnp.float32) * s, 'shared_down_w': jax.random.normal(ks[4], (HIDDEN, SHARED_INTER), dtype=jnp.float32) * s, 'w13': jax.random.normal(ks[5], (NUM_EXPERTS, 2 * MOE_INTER, HIDDEN), dtype=jnp.float32) * s, 'w2': jax.random.normal(ks[6], (NUM_EXPERTS, HIDDEN, MOE_INTER), dtype=jnp.float32) * s}
    _L0_ffn_in = _L0_ffn_setup()
    _d = {'L0_attn_x': _L0_attn_in['x'], 'L0_attn_qkv': _L0_attn_in['qkv'], 'L0_attn_o_proj': _L0_attn_in['o_proj'], 'L0_attn_gamma': _L0_attn_in['gamma'], 'L0_attn_beta': _L0_attn_in['beta'], 'L0_ffn_gate_w': _L0_ffn_in['gate_w'], 'L0_ffn_shared_gate_w': _L0_ffn_in['shared_gate_w'], 'L0_ffn_shared_gate_up_w': _L0_ffn_in['shared_gate_up_w'], 'L0_ffn_shared_down_w': _L0_ffn_in['shared_down_w'], 'L0_ffn_w13': _L0_ffn_in['w13'], 'L0_ffn_w2': _L0_ffn_in['w2']}
    _x0 = _d['L0_attn_x']
    _d['L0_attn_x'] = jax.random.normal(jax.random.fold_in(jax.random.key(seed), 1), (4, 1024, 256), dtype=_x0.dtype)
    del _x0
    return _d

def reference(L0_attn_x, L0_attn_qkv, L0_attn_o_proj, L0_attn_gamma, L0_attn_beta, L0_ffn_gate_w, L0_ffn_shared_gate_w, L0_ffn_shared_gate_up_w, L0_ffn_shared_down_w, L0_ffn_w13, L0_ffn_w2):

    def _L0_attn_ref(x, qkv, o_proj, gamma, beta):
        import jax, jax.numpy as jnp
        import numpy as np
        HIDDEN = 256
        KEY = 256
        EPS = 1e-05
        residual = x
        mu = jnp.mean(x, axis=-1, keepdims=True)
        var = jnp.mean((x - mu) ** 2, axis=-1, keepdims=True)
        x_norm = (x - mu) / jnp.sqrt(var + EPS) * gamma + beta
        q = x_norm @ qkv[:, :KEY]
        k = x_norm @ qkv[:, KEY:2 * KEY]
        v = x_norm @ qkv[:, 2 * KEY:]
        scale = 1.0 / jnp.sqrt(jnp.float32(KEY))
        scores = jnp.einsum('bsk,btk->bst', q, k) * scale
        S_len = x.shape[1]
        causal = jnp.tril(jnp.ones((S_len, S_len), dtype=bool))
        scores = jnp.where(causal[None], scores, -jnp.inf)
        attn = jax.nn.softmax(scores, axis=-1)
        out = attn @ v
        out = out @ o_proj
        return out + residual

    def _L0_ffn_ref(hidden_states, gate_w, shared_gate_w, shared_gate_up_w, shared_down_w, w13, w2):
        import jax, jax.numpy as jnp
        import numpy as np
        HIDDEN = 256
        NUM_EXPERTS = 8
        TOP_K = 2
        MOE_INTER = 176
        SHARED_INTER = 704

        def _silu_and_mul(gu):
            i = gu.shape[-1] // 2
            return jax.nn.silu(gu[:, :i]) * gu[:, i:]
        orig_shape = hidden_states.shape
        x = hidden_states.reshape(-1, orig_shape[-1])
        shared = _silu_and_mul(x @ shared_gate_up_w.T) @ shared_down_w.T
        shared = shared * jax.nn.sigmoid(x @ shared_gate_w.T)
        router_logits = x @ gate_w.T
        probs = jax.nn.softmax(router_logits.astype(jnp.float32), axis=-1)
        routing_weights, selected_experts = jax.lax.top_k(probs, TOP_K)
        combined = jnp.zeros(x.shape, dtype=jnp.float32)
        E = w13.shape[0]
        for e in range(E):
            w_e = jnp.where(selected_experts == e, routing_weights, 0.0).sum(-1)
            h = _silu_and_mul(x @ w13[e].T) @ w2[e].T
            combined = combined + w_e[:, None] * h.astype(jnp.float32)
        out = shared + combined.astype(x.dtype)
        return out.reshape(orig_shape)
    x = L0_attn_x
    x = x + _L0_attn_ref(_layernorm(x, axis=-1), L0_attn_qkv, L0_attn_o_proj, L0_attn_gamma, L0_attn_beta)
    x = x + _L0_ffn_ref(_layernorm(x, axis=-1), L0_ffn_gate_w, L0_ffn_shared_gate_w, L0_ffn_shared_gate_up_w, L0_ffn_shared_down_w, L0_ffn_w13, L0_ffn_w2)
    return x

_drawn_inputs = setup_inputs


def setup_inputs(seed=0):
    import zlib

    import numpy as np

    out = dict(_drawn_inputs(seed))
    spreads = {'L0_attn_gamma': (1.0, 0.6), 'L0_attn_beta': (0.0, 0.565)}
    factors = {'L0_attn_o_proj': 2.682,
     'L0_ffn_gate_w': 8.0,
     'L0_ffn_shared_gate_w': 8.0,
     'L0_ffn_shared_gate_up_w': 7.926,
     'L0_ffn_shared_down_w': 7.932,
     'L0_ffn_w13': 8.0,
     'L0_ffn_w2': 8.0}
    for name, (base, spread) in spreads.items():
        noise = np.random.default_rng([zlib.crc32(name.encode()), seed]).standard_normal(out[name].shape)
        drawn = base * np.exp(spread * noise) if base else spread * noise
        out[name] = jnp.asarray(drawn.astype(out[name].dtype))
    for name, factor in factors.items():
        out[name] = (out[name] * factor).astype(out[name].dtype)
    return out
```

```python
import math

import concourse.bass as bass
from concourse import mybir

B, S, D = 4, 1024, 256
T = B * S
P = 128
NP = T // (2 * P)
SLOTS = S // (2 * P)
KD = D // P
F = 704
UNITS = 6
NE = 8
FE = 176
FH = FE // 2
ROWS = T + P
RW = 2 * D + 2
SPARE = 2 * NE
NBLK = (2 * T + NE * (P - 1)) // P + 1
RING = 8
PARTS = 4
EPS = 1e-5
SCALE = 1.0 / math.sqrt(D)
UP = 1024.0
MASKED = -1e30


def program(nc, x, wqT, wkT, wvT, wo, gamma_beta, router, wgu, wsd, w13, w2, out):
    dt = mybir.dt
    f32, f32r, f16, bf16, i32 = dt.float32, dt.float32r, dt.float16, dt.bfloat16, dt.int32
    ALU, ACT, AX = mybir.AluOpType, mybir.ActivationFunctionType, mybir.AxisListType
    ds = bass.ds

    row_tab = nc.dram_tensor("row_tab", ((NE * ROWS + (SPARE - NE) * P), RW), f16, kind="Internal").ap()
    exp_tab = nc.dram_tensor("exp_tab", (2 * T + SPARE * P, D), f32, kind="Internal").ap()
    xs_tab = nc.dram_tensor("xs_tab", (T, D), f32, kind="Internal").ap()

    top = [-(-nc.sbuf_base // 64) * 64]
    size = {f32: 4, f32r: 4, f16: 2, bf16: 2, i32: 4}

    def place(name, shape, dtype, at=None):
        n = size[dtype]
        for d in shape[1:]:
            n *= d
        where = top[0] if at is None else at
        if at is None:
            top[0] += -(-n // 32) * 32
        return nc.alloc_sbuf_tensor_at(name, shape, dtype, offset=where)

    base_kv = top[0]
    xT = place("xT", [P, 2, KD, S], f32r)
    vp = place("vp", [P, 2, 2 * SLOTS, D], f32r)
    base_att = top[0]
    qT = place("qT", [P, 2, 2, KD, 2 * P], f32r)
    p32 = place("p32", [P, S], f32)
    p16 = place("p16", [P, 2, S], f16)
    pT = place("pT", [P, 2, 2 * SLOTS, P], f32r)
    base_ffn = top[0]
    yT = place("yT", [P, 2, KD, 2 * P], f32r)
    hT = place("hT", [P, 2, UNITS, 2 * P], f32r)
    x_in = place("x_in", [P, 2, 2, D], f32)
    xz = place("xz", [P, 2, 2, D], f32)
    base_x1 = top[0]
    x1 = place("x1", [P, 4, 2, D], f32)
    n32 = place("n32", [P, 2, D], f32)
    n16 = place("n16", [P, 2, 2, D], f16)
    y16 = place("y16", [P, 2, 2, 2, RW], f16)
    xg = place("xg", [P, KD, 2 * P], f32)
    th = place("th", [P, 2, 2 * P], f32)
    h32 = place("h32", [P, 2, 2 * P], f32)
    stage = place("stage", [P, 3, F], f32)
    wA = place("wA", [P, 2, KD, D], f32r)
    wV = place("wV", [P, 2, KD, D], f32r)
    wR = place("wR", [P, 2, KD, 10], f32r)
    wG = place("wG", [P, 2, KD, 2 * F], f32r)
    wS = place("wS", [P, 2, UNITS, D], f32r)
    wE = place("wE", [P, 2, NE, KD, 2 * FE], f32r)
    ident16 = place("ident16", [P, P], f16)
    identf = place("identf", [P, P], f32)
    identr = place("identr", [P, P], f32r)
    mask = place("mask", [P, 2, 2 * P], f32r)
    upper = place("upper", [P, P], bf16)
    ones = place("ones", [P, P], bf16)
    idtab = place("idtab", [P, NP, 2, 2], i32)
    wts = place("wts", [P, NP, 2, 2], f32)
    w8 = place("w8", [P, 2, NE], f32)
    eoff = place("eoff", [P, 2, NE], f32)
    gam = place("gam", [P, 2, KD], f32)
    half = place("half", [P, 4], f32)
    st = place("st", [P, 4, 6], f32)
    mv1 = place("mv1", [P, 2, 2, 2], f32)
    mv2 = place("mv2", [P, 2, 2, 2], f32)
    b1 = place("b1", [P, 2, 2], f32)
    r1 = place("r1", [P, 2, 2, 2], f32)
    b2 = place("b2", [P, 2], f32)
    r2 = place("r2", [P, 2, 2], f32)
    rmax = place("rmax", [P, 2], f32)
    nmax = place("nmax", [P, 2], f32)
    rsum = place("rsum", [P, 2], f32)
    idle = place("idle", [P, 2], f32)
    idle_dve = place("idle_dve", [P, 1], f32)
    gam_in = place("gam_in", [P, 2, KD], f32)
    r_in = place("r_in", [P, KD, 10], f32)
    rinv = place("rinv", [P, 2], f32)
    lg = place("lg", [P, 2, 10], f32)
    sh = place("sh", [P, 2, NE], f32)
    ex = place("ex", [P, 2, NE], f32)
    pr = place("pr", [P, 2, NE], f32)
    ca = place("ca", [P, 2, NE], f32)
    cb = place("cb", [P, 2, NE], f32)
    one = place("one", [P, 2, 2, NE], f32)
    small = place("small", [P, 8, 2], f32)
    vtmp = place("vtmp", [P, 2, 2], f32)
    tg = place("tg", [P, 2], f32)
    sg = place("sg", [P, 2, 2], f32)
    mk = place("mk", [P, 2, NE], bf16)
    cum = place("cum", [P, 2, 3, NE], bf16)
    dd = place("dd", [P, 2, NE], f32)
    df = place("df", [P, 2, 2], f32)
    di = place("di", [P, 2, 2, 2], i32)
    tc = place("tc", [P, 12, NE], f32)
    tci = place("tci", [P, NE], i32)
    blk = place("blk", [1, NBLK], f32)
    tab_e = place("tab_e", [1, NBLK], i32)
    tab_r = place("tab_r", [1, NBLK], i32)
    pad_i = place("pad_i", [1, NE], i32)
    assert top[0] <= nc.sbuf_usable_end, (top[0], nc.sbuf_usable_end)
    base_h = base_ffn + 2 * KD * 2 * P * 4
    w_raw = [place(f"w_raw{i}", [P, KD, D], f32, at=base_h + i * KD * D * 4) for i in range(4)]
    maskf = place("maskf", [P, 2, 2 * P], f32, at=base_att + 8192)
    upf = place("upf", [P, P], f32, at=base_att + 8192 + 4 * 512)
    w2s = place("w2s", [P, 2, NE, 2, D], f32r, at=base_kv)
    at = [base_att]

    def later(name, shape, dtype, room):
        n = size[dtype]
        for d in shape[1:]:
            n *= d
        t = place(name, shape, dtype, at=at[0])
        at[0] += -(-n // 32) * 32
        assert at[0] <= room
        return t

    rows = later("rows", [P, RING, RW], f16, base_ffn)
    rT = later("rT", [P, 2, 2, KD, P], f32r, base_ffn)
    eth = later("eth", [P, 2, FE], f32, base_ffn)
    eh = later("eh", [P, 2, FE], f32, base_ffn)
    ehT = later("ehT", [P, 2, 2, 2, P], f32r, base_ffn)
    pad_rows = later("pad_rows", [P, 2 * D], f16, base_ffn)
    pad_ids = later("pad_ids", [P, SPARE], i32, base_ffn)
    eo = place("eo", [P, RING, D], f32, at=base_x1)
    at = [base_ffn + 16384]
    tb = later("tb", [1, NBLK, NE], f32, base_ffn + 24576)
    tbb = later("tbb", [1, NBLK, NE], f32, base_ffn + 24576)
    tw = later("tw", [1, 4, NBLK], f32, base_ffn + 24576)
    at = [base_ffn]
    cx = later("cx", [P, PARTS, 3, 2, D], f32, base_ffn + 24576)

    scores = nc.alloc_psum_tensor("scores", [P, 2 * 512], f32)
    banks = [scores[:, 0:512], scores[:, 512:1024]]
    banks += [nc.alloc_psum_tensor(f"bank{i}", [P, 512], f32)[:, :] for i in range(2, 8)]
    s_banks = banks[0:2]
    t_banks = banks[2:4]
    o_bank, x_bank = banks[4], banks[7]
    g_banks = banks[5:7]

    sems = {}

    def sem(name):
        if name not in sems:
            sems[name] = nc.alloc_semaphore(name)
        return sems[name]

    def wait(e, name, n):
        if isinstance(n, int) and n <= 0:
            return
        e.wait_ge(sem(name), n)

    def chained(e, name, per, n):
        count = [0]

        def link(ins):
            count[0] += 1
            ins.then_inc(sem(name), 1)
            wait(e, name, n * per + count[0])
        return link, count

    def bc(ap, n):
        return ap.rearrange("p (a o) -> p a o", o=1).to_broadcast([P, ap.shape[1], n])

    def products(pe, dst, lhs, rhs, first=True, last=True):
        for n, (a, b) in enumerate(((0, 0), (0, 1), (1, 0))):
            ins = pe.matmul(dst, lhs(a), rhs(b), start=first and n == 0, stop=last and n == 2)
        return ins

    def slots(e, slot):
        for j in range(SLOTS):
            slot(0, j)
        with e.Fori(1, B) as b:
            for j in range(SLOTS):
                slot(b, j)

    chunks = []
    for k in range(KD):
        for c in (0, F):
            chunks.append((wgu[k * P:(k + 1) * P, c:c + F], lambda hl, k=k, c=c: wG[:, hl, k, c:c + F], F, 0, F))
    for k, n in ((0, 2), (2, 2), (4, 1)):
        chunks.append((wsd[k * P:(k + n) * P, :], lambda hl, k=k, n=n: wS[:, hl, k:k + n, :], n * D, 0, D))
    chunks.append((wsd[5 * P:F, :], lambda hl: wS[64:P, hl, 5:6, :], D, 64, D))
    N_FFN = len(chunks)
    for i in range(NE):
        chunks.append((w13[i], lambda hl, i=i: wE[:, hl, i, :, :], 2 * 2 * FE, 0, 2 * FE))
    N_W13 = len(chunks)
    for i in range(NE):
        chunks.append((w2[i], lambda hl, i=i: w2s[0:FH, hl, i, :, :], 2 * D, 0, D))
    NW = len(chunks)

    def staged(n):
        src, dst, width, p0, inner = chunks[n]
        rows_ = dst(0).shape[0]
        return stage[p0:p0 + rows_, n % 3, 0:width].rearrange("p (k n) -> p k n", n=inner)

    def halves(n, hl):
        dst = chunks[n][1](hl)
        return dst.rearrange("p (k n) -> p k n", k=1) if len(dst.shape) == 2 else dst

    turns = {0: range(0, N_FFN), 1: range(N_FFN, N_FFN + 3), 2: range(N_FFN + 3, N_FFN + 6),
             3: range(N_FFN + 6, N_W13)}

    with nc.Block() as block:

        @block.sync
        def _(sp):
            def first_row(pair):
                return pair * 2 * P if isinstance(pair, int) else sp.snap(pair * 2 * P)

            def load_x(pair, par, *waits):
                row = first_row(pair)
                for w in waits:
                    wait(sp, *w)
                sp.dma_start(x_in[:, par, :, :],
                             x[ds(row, 2 * P), :].rearrange("(t p) d -> p t d", p=P)
                             ).then_inc(sem(f"x_loaded{par}"), 16)

            load_x(0, 0)
            sp.dma_start(w_raw[0][:, :, :], wqT.rearrange("(k p) n -> p k n", p=P)).then_inc(sem("qkv_loaded"), 16)
            sp.dma_start(w_raw[1][:, :, :], wkT.rearrange("(k p) n -> p k n", p=P)).then_inc(sem("qkv_loaded"), 16)
            sp.dma_start(w_raw[2][:, :, :], wvT.rearrange("(k p) n -> p k n", p=P)).then_inc(sem("qkv_loaded"), 16)
            sp.dma_start(w_raw[3][:, :, :], wo.rearrange("(k p) n -> p k n", p=P)).then_inc(sem("qkv_loaded"), 16)
            sp.dma_start(gam_in[:, :, :], gamma_beta).then_inc(sem("gam_loaded"), 16)
            sp.dma_start(r_in[:, :, :], router.rearrange("(k p) n -> p k n", p=P)).then_inc(sem("gam_loaded"), 16)
            load_x(1, 1)
            def load_chunk(n):
                wait(sp, "w_split", n - 2)
                rows_ = staged(n).shape[0]
                sp.dma_start(staged(n), chunks[n][0].rearrange("(k p) n -> p k n", p=rows_)
                             ).then_inc(sem(f"w_loaded{n % 3}"), 16)

            for n in range(3):
                load_chunk(n)
            chunk = [3]

            def slot(b, j):
                s = b * SLOTS + j
                load_x((s + 2) % NP, j % 2, ("xz_done", s + 1))
                if not isinstance(s, int) or s >= 2:
                    store_xs(b, j)
                if s in turns if isinstance(s, int) else False:
                    while chunk[0] < min(turns[s].stop + 3, N_W13):
                        load_chunk(chunk[0])
                        chunk[0] += 1

            def store_xs(b, j):
                p2 = b * SLOTS + j - 2
                row = first_row(p2)
                wait(sp, "xs_done", 2 * p2 + 2)
                sp.dma_start(xs_tab[ds(row, 2 * P), :].rearrange("(t p) d -> p t d", p=P),
                             x1[:, (j + 2) % 4, :, :]).then_inc(sem(f"xs_stored{j % 2}"), 16)

            slots(sp, slot)
            for j in (0, 1):
                store_xs(B, j)
            for n in range(N_W13, NW):
                load_chunk(n)
            def store_pads(n, row):
                sp.dma_start(row_tab[ds(row, P), 0:2 * D], pad_rows[:, :]).then_inc(sem("pads_stored"), 16)
                sp.dma_start(row_tab[ds(row, P), 2 * D:RW], pad_ids[:, n:n + 1].bitcast(f16)
                             ).then_inc(sem("pads_stored"), 16)

            sp.wait_ge(sem("pad_rows_built"), 1)
            for n in range(NE, SPARE):
                store_pads(n, NE * ROWS + (n - NE) * P)
            sp.wait_ge(sem("pad_ready"), 1)
            for n in range(NE):
                store_pads(n, sp.value_load(pad_i[0:1, n:n + 1], min_val=0, max_val=NE * ROWS - P))
            sp.wait_ge(sem("pads_stored"), 32 * SPARE)
            sp.wait_ge(sem("table_done"), 1)
            for par in (0, 1):
                sp.wait_ge(sem(f"rows_stored{par}"), 64 * (NP // 2))

            def load_rows(n, u):
                r = sp.value_load(tab_r[0:1, ds(n, 1)], min_val=0, max_val=NE * ROWS + (SPARE - NE - 1) * P)
                wait(sp, f"scattered{u}", (n - u) * 16 // RING if isinstance(n, int) else (n - u) * 2)
                sp.dma_start(rows[:, u, :], row_tab[ds(r, P), :]).then_inc(sem(f"rows_loaded{u}"), 16)

            sp.wait_ge(sem("vlo_done"), NP + 1)
            for u in range(RING):
                load_rows(u, u)
            with sp.Fori(1, NBLK // RING) as i:
                for u in range(RING):
                    load_rows(i * RING + u, u)
            sp.wait_ge(sem("xs_done"), 2 * NP)
            for par in (0, 1):
                sp.wait_ge(sem(f"xs_stored{par}"), 16 * (NP // 2))
            for u in range(RING):
                sp.wait_ge(sem(f"scattered{u}"), 16 * (NBLK // RING))

            def load_parts(pair, u, *waits):
                own = [first_row(pair), first_row(pair), first_row(pair + T // (2 * P))]
                for w in waits:
                    wait(sp, *w)
                for k, src in enumerate((xs_tab, exp_tab, exp_tab)):
                    sp.dma_start(cx[:, u, k, :, :],
                                 src[ds(own[k], 2 * P), :].rearrange("(t p) d -> p t d", p=P)
                                 ).then_inc(sem(f"parts_loaded{u}"), 16)

            def store_out(pair, u):
                row = first_row(pair)
                sp.wait_ge(sem("combined"), pair + 1)
                sp.dma_start(out[ds(row, 2 * P), :].rearrange("(t p) d -> p t d", p=P),
                             cx[:, u, 0, :, :]).then_inc(sem(f"out_stored{u}"), 16)

            for u in range(PARTS):
                load_parts(u, u)
            with sp.Fori(0, NP // PARTS - 1) as i:
                for u in range(PARTS):
                    store_out(i * PARTS + u, u)
                for u in range(PARTS):
                    load_parts(i * PARTS + PARTS + u, u, (f"out_stored{u}", i * 16 + 16))
            for u in range(PARTS):
                store_out(NP - PARTS + u, u)
            for u in range(PARTS):
                sp.wait_ge(sem(f"out_stored{u}"), 16 * (NP // PARTS))

        @block.tensor
        def _(pe):
            X16 = x_bank.bitcast(f16)

            def qk(b, j, a):
                s = b * SLOTS + j
                wait(pe, "qlo_done", s + 1)
                wait(pe, "xlo_done", s + 1)
                wait(pe, "pexp_done", 2 * s + a)
                if a == 0:
                    wait(pe, "prefix_read", s - 1)
                else:
                    wait(pe, "logits_read", s)
                n = (j + 1) * 2 * P
                for c in range(0, n, 512):
                    w = min(512, n - c)
                    dst = s_banks[c // 512][:, 0:w]
                    for k in range(KD):
                        ins = products(pe, dst,
                                       lambda hl: qT[:, hl, j % 2, k, a * P:(a + 1) * P],
                                       lambda hl: xT[:, hl, k, c:c + w],
                                       first=k == 0, last=k == KD - 1 and c + w < n)
                    if c + w == n:
                        ins = pe.matmul(s_banks[c // 512][:, w - 2 * P:w], identr[:, :], mask[:, a, :],
                                        start=False, stop=True)
                ins.then_inc(sem("qk_done"), 1)

            def down(b, j, t):
                p = b * SLOTS + j - 2
                wait(pe, "hlo_done", (UNITS - 1) * (p + 1))
                wait(pe, "hlast_done", p + 1)
                wait(pe, "hhi_done", UNITS * p + UNITS)
                wait(pe, "pThi_done" if t == 0 else "pTlo_done", min(2 * (p + 2), 2 * NP) if isinstance(p, int) else 2 * (p + 2))
                if p == NP - 1 if isinstance(p, int) else False:
                    pe.wait_ge(sem("xs_done"), 2 * NP - 2)
                for k in range(UNITS):
                    q0 = 64 if k == UNITS - 1 else 0
                    ins = products(pe, t_banks[t][:, 0:D],
                                   lambda hl: hT[q0:P, hl, k, t * P:(t + 1) * P],
                                   lambda hl: wS[q0:P, hl, k, :],
                                   first=k == 0, last=k == UNITS - 1)
                ins.then_inc(sem("down_done"), 1)

            def transpose_y(b, j):
                p = b * SLOTS + j - 1
                wait(pe, "vlo_done", p + 2)
                wait(pe, "y16lo_done", p + 1)
                for hl in range(2):
                    for k in range(KD):
                        for t in range(2):
                            o = hl * 512 + k * 256 + t * P
                            src = y16[:, (j + 1) % 2, 0, t, hl * D + k * P:hl * D + (k + 1) * P]
                            ins = pe.transpose(X16[:, o:o + P], src, ident16[:, :])
                ins.then_inc(sem("yT_tp"), 1)

            def transpose_x(b, j):
                q = b * SLOTS + j + 1
                wait(pe, "yT_done", q - 1)
                wait(pe, "vlo_done", q)
                wait(pe, "n16lo_done", q + 1)
                for hl in range(2):
                    for k in range(KD):
                        for t in range(2):
                            o = hl * 512 + k * 256 + t * P
                            ins = pe.transpose(X16[:, o:o + P], n16[:, hl, t, k * P:(k + 1) * P], ident16[:, :])
                ins.then_inc(sem("xT_tp"), 1)

            def transpose_p(b, j, a):
                g = (b * SLOTS + j) * 2 + a
                wait(pe, "plo_done", g + 1)
                if a == 0:
                    wait(pe, "xs_done", g - 2)
                wait(pe, "pThi_done", g)
                wait(pe, "pTlo_done", g)
                for hl in range(2):
                    for kb in range(2 * j + a + 1):
                        ins = pe.transpose(t_banks[hl].bitcast(f16)[:, kb * P:(kb + 1) * P],
                                           p16[:, hl, kb * P:(kb + 1) * P], ident16[:, :])
                    ins.then_inc(sem("pT_tp"), 1)

            def logits(b, j):
                p = b * SLOTS + j - 1
                wait(pe, "yT_done", p + 1)
                wait(pe, "prefix_read", p)
                for t in range(2):
                    for k in range(KD):
                        ins = products(pe, s_banks[0][:, t * 10:(t + 1) * 10],
                                       lambda hl: yT[:, hl, k, t * P:(t + 1) * P],
                                       lambda hl: wR[:, hl, k, :], first=k == 0, last=k == KD - 1)
                ins.then_inc(sem("logits_done"), 1)

            def prefix(b, j):
                p = b * SLOTS + j - 1
                wait(pe, "mask_done", p + 1)
                wait(pe, "logits_read", p + 1)
                dst = s_banks[0][:, 0:2 * NE]
                pe.matmul(dst, upper[:, :], mk[:, :, :].rearrange("p t e -> p (t e)"), start=True, stop=False)
                pe.matmul(dst, ones[:, :], cum[:, (j + 1) % 2, 0:2, :].rearrange("p t e -> p (t e)"),
                          start=False, stop=True).then_inc(sem("prefix_done"), 1)

            def pv(b, j, a):
                g = (b * SLOTS + j) * 2 + a
                wait(pe, "pThi_done", g + 1)
                wait(pe, "pTlo_done", g + 1)
                wait(pe, "vlo_done", b * SLOTS + j + 1)
                wait(pe, "x1_done", g)
                n = 2 * j + a + 1
                for kb in range(n):
                    ins = products(pe, o_bank[:, a * D:(a + 1) * D],
                                   lambda hl: pT[:, hl, kb, :], lambda hl: vp[:, hl, kb, :],
                                   first=kb == 0, last=kb == n - 1)
                ins.then_inc(sem("pv_done"), 1)

            def unit(b, j, u):
                p = b * SLOTS + j - 1
                wait(pe, "yT_done", p + 1)
                wait(pe, "h_done", UNITS * p + u - 1)
                g = g_banks[u % 2]
                for i in range(1 if u == UNITS - 1 else 2):
                    for k in range(KD):
                        c = u * 2 * P + i * P
                        ins = products(pe, g[:, i * 256:(i + 1) * 256],
                                       lambda hl: wG[:, hl, k, c:c + P], lambda hl: yT[:, hl, k, :],
                                       first=k == 0, last=k == KD - 1)
                ins.then_inc(sem("gu_done"), 1)

            def q_proj(b, j):
                q = b * SLOTS + j + 1
                wait(pe, "xlo_done", q + 1)
                c = ((j + 1) % SLOTS) * 2 * P
                for m in range(KD):
                    for k in range(KD):
                        ins = products(pe, x_bank[:, m * 256:(m + 1) * 256],
                                       lambda hl: wA[:, hl, k, m * P:(m + 1) * P],
                                       lambda hl: xT[:, hl, k, c:c + 2 * P], first=k == 0, last=k == KD - 1)
                ins.then_inc(sem("q_done"), 1)

            def v_proj(b, j):
                q = b * SLOTS + j + 1
                wait(pe, "qlo_done", q + 1)
                c = ((j + 1) % SLOTS) * 2 * P
                for t in range(2):
                    for k in range(KD):
                        ins = products(pe, x_bank[:, t * 256:(t + 1) * 256],
                                       lambda hl: xT[:, hl, k, c + t * P:c + (t + 1) * P],
                                       lambda hl: wV[:, hl, k, :], first=k == 0, last=k == KD - 1)
                ins.then_inc(sem("v_done"), 1)

            pe.wait_ge(sem("qkv_loaded"), 64)
            for n, (l, r) in enumerate(((0, 1), (2, 3))):
                for m in range(KD):
                    for k in range(KD):
                        ins = pe.matmul(banks[n][:, m * 256:(m + 1) * 256], w_raw[l][:, k, m * P:(m + 1) * P],
                                        w_raw[r][:, k, :], start=k == 0, stop=k == KD - 1)
                ins.then_inc(sem("wprod_done"), 1)
            pe.wait_ge(sem("consts_done"), 1)
            transpose_x(0, -1)
            pe.wait_ge(sem("wprod_split"), 2)
            q_proj(0, -1)
            v_proj(0, -1)

            def slot(b, j, last=False):
                s = b * SLOTS + j
                known = isinstance(s, int)
                if not last:
                    qk(b, j, 0)
                if not known or s >= 2:
                    down(b, j, 0)
                    down(b, j, 1)
                if not known or s >= 1:
                    transpose_y(b, j)
                if not last:
                    transpose_p(b, j, 0)
                if not known or s >= 1:
                    logits(b, j)
                if not last:
                    pv(b, j, 0)
                    qk(b, j, 1)
                    transpose_x(b, j)
                if not known or s >= 1:
                    if known and s == 1:
                        pe.wait_ge(sem("w_split"), N_FFN)
                    unit(b, j, 0)
                    unit(b, j, 1)
                if not last:
                    transpose_p(b, j, 1)
                if not known or s >= 1:
                    prefix(b, j)
                    unit(b, j, 2)
                    unit(b, j, 3)
                if not last:
                    q_proj(b, j)
                    pv(b, j, 1)
                    v_proj(b, j)
                if not known or s >= 1:
                    unit(b, j, 4)
                    unit(b, j, 5)

            slots(pe, slot)
            slot(B, 0, last=True)
            pe.wait_ge(sem("prefix_read"), NP)
            pe.matmul(s_banks[0][:, 0:NE], ones[:, :], cum[:, (NP - 1) % 2, 2, :], start=True, stop=True
                      ).then_inc(sem("count_done"), 1)
            down(B, 1, 0)
            down(B, 1, 1)

            def rows_T(n, u, m):
                wait(pe, f"rows_loaded{u}", (m + 1) * 16)
                wait(pe, "rT_done", n - 1)
                for hl in range(2):
                    for k in range(KD):
                        o = hl * 256 + k * P
                        ins = pe.transpose(banks[u % 2].bitcast(f16)[:, o:o + P],
                                           rows[:, u, hl * D + k * P:hl * D + (k + 1) * P], ident16[:, :])
                ins.then_inc(sem("rT_tp"), 1)

            def expert_gu(n, u):
                e_ = pe.value_load(tab_e[0:1, ds(n, 1)], min_val=0, max_val=NE - 1)
                wait(pe, "rT_done", n + 1)
                wait(pe, "eh_done", n - 1)
                for k in range(KD):
                    ins = products(pe, banks[2 + u % 2][:, 0:2 * FE], lambda hl: rT[:, u % 2, hl, k, :],
                                   lambda hl: wE[:, hl, ds(e_, 1), k, :].rearrange("p a n -> p (a n)"),
                                   first=k == 0, last=k == KD - 1)
                ins.then_inc(sem("egu_done"), 1)

            def inner_T(n, u):
                wait(pe, "eh_done", n + 1)
                wait(pe, "ehT_done", n - 1)
                for c in range(2):
                    ins = pe.transpose(banks[4 + u % 2][0:FH, c * P:(c + 1) * P],
                                       eh[:, u % 2, c * FH:(c + 1) * FH], identf[:, :])
                ins.then_inc(sem("ehT_tp"), 1)

            def expert_down(n, u):
                e_ = pe.value_load(tab_e[0:1, ds(n, 1)], min_val=0, max_val=NE - 1)
                wait(pe, "ehT_done", n + 1)
                wait(pe, "eo_done", n - 1)
                for c in range(2):
                    ins = products(pe, banks[6 + u % 2][:, 0:D], lambda hl: ehT[0:FH, u % 2, hl, c, :],
                                   lambda hl: w2s[0:FH, hl, ds(e_, 1), c, :].rearrange("p a n -> p (a n)"),
                                   first=c == 0, last=c == 1)
                ins.then_inc(sem("edown_done"), 1)

            def step(n, u, m):
                known = isinstance(n, int)
                if not known or n + 1 < NBLK:
                    rows_T(n + 1, (u + 1) % RING, m + (u + 1) // RING)
                if not known or n < NBLK:
                    expert_gu(n, u)
                if not known or 0 <= n - 1 < NBLK:
                    inner_T(n - 1, (u - 1) % RING)
                if not known or 0 <= n - 2 < NBLK:
                    expert_down(n - 2, (u - 2) % RING)

            pe.wait_ge(sem("w_split"), NW)
            pe.wait_ge(sem("xs_done"), 2 * NP)
            rows_T(0, 0, 0)
            for n in range(RING):
                step(n, n, 0)
            with pe.Fori(1, NBLK // RING - 1) as i:
                for u in range(RING):
                    step(i * RING + u, u, i)
            for n in range(NBLK - RING, NBLK + 2):
                step(n, n % RING, n // RING)

        @block.scalar
        def _(act):
            X16 = x_bank.bitcast(f16)

            def exps(b, j, a):
                g = (b * SLOTS + j) * 2 + a
                n = 2 * j + a + 1
                wait(act, "nmax_done", g + 1)
                wait(act, "pT_tp", 2 * g)
                n *= P
                args = (scores[:, 0:n], ACT.Exp, nmax[:, a:a + 1], SCALE)
                act.activation(p16[:, 0, 0:n], *args)
                act.activation(p32[:, 0:n], *args, accum_out=rsum[:, a:a + 1]).then_inc(sem("pexp_done"), 1)

            def y_T(b, j):
                p = b * SLOTS + j - 1
                wait(act, "yT_tp", p + 1)
                wait(act, "gu_done", UNITS * p)
                act.activation(yT[:, :, :, :].rearrange("p h k n -> p (h k n)"), X16[:, :], ACT.Copy,
                               scale=1.0 / UP).then_inc(sem("yT_done"), 1)

            def p_T(b, j, a):
                g = (b * SLOTS + j) * 2 + a
                n = 2 * j + a + 1
                wait(act, "pT_tp", 2 * g + 1)
                wait(act, "pv_done", g)
                act.activation(pT[:, 0, 0:n, :].rearrange("p k q -> p (k q)"),
                               t_banks[0].bitcast(f16)[:, 0:n * P], ACT.Copy).then_inc(sem("pThi_done"), 1)

            def route_acts(b, j):
                p = b * SLOTS + j - 1
                wait(act, "shifted_done", p + 1)
                act.activation(tg[:, :], lg[:, :, 8], ACT.Tanh, scale=0.5)
                act.activation(ex[:, :, :], sh[:, :, :], ACT.Exp).then_inc(sem("rexp_done"), 1)

            def x_gamma(b, j):
                q = b * SLOTS + j + 1
                wait(act, "xT_tp", q + 1)
                wait(act, "xlo_done", q)
                for k in range(KD):
                    ins = act.activation(xg[:, k, :], X16[:, k * 256:(k + 1) * 256], ACT.Identity,
                                         scale=gam[:, 0, k:k + 1], bias=gam[:, 1, k:k + 1])
                ins.then_inc(sem("xg_done"), 1)

            def x_hi(b, j):
                q = b * SLOTS + j + 1
                c = ((j + 1) % SLOTS) * 2 * P
                wait(act, "xsum_done", q + 1)
                act.activation(xT[:, 0, :, c:c + 2 * P], xg[:, :, :], ACT.Copy).then_inc(sem("xhi_done"), 1)

            def q_hi(b, j):
                q = b * SLOTS + j + 1
                wait(act, "q_done", q + 1)
                act.activation(qT[:, 0, (j + 1) % 2, :, :].rearrange("p k n -> p (k n)"), x_bank[:, :], ACT.Copy
                               ).then_inc(sem("qhi_done"), 1)

            def v_hi(b, j):
                q = b * SLOTS + j + 1
                c = ((j + 1) % SLOTS) * 2
                wait(act, "v_done", q + 1)
                act.activation(vp[:, 0, c:c + 2, :].rearrange("p k n -> p (k n)"), x_bank[:, :], ACT.Copy
                               ).then_inc(sem("vhi_done"), 1)

            def unit_tanh(b, j, u):
                p = b * SLOTS + j - 1
                wait(act, "gu_done", UNITS * p + u + 1)
                wait(act, "h_done", UNITS * p + u - 1)
                m = 64 if u == UNITS - 1 else P
                act.activation(th[0:m, u % 2, :], g_banks[u % 2][0:m, 0:256], ACT.Tanh, scale=0.5
                               ).then_inc(sem("th_done"), 1)

            def h_hi(b, j, u):
                p = b * SLOTS + j - 1
                wait(act, "h_done", UNITS * p + u + 1)
                wait(act, "down_done", 2 * p)
                q0 = 64 if u == UNITS - 1 else 0
                act.activation(hT[q0:P, 0, u, :], h32[q0:P, u % 2, :], ACT.Copy).then_inc(sem("hhi_done"), 1)

            def slot(b, j, last=False):
                s = b * SLOTS + j
                behind = not isinstance(s, int) or s >= 1
                if not last:
                    exps(b, j, 0)
                if behind:
                    y_T(b, j)
                if not last:
                    p_T(b, j, 0)
                if behind:
                    route_acts(b, j)
                if not last:
                    exps(b, j, 1)
                    x_gamma(b, j)
                if behind:
                    unit_tanh(b, j, 0)
                    unit_tanh(b, j, 1)
                    h_hi(b, j, 0)
                if not last:
                    x_hi(b, j)
                    p_T(b, j, 1)
                if behind:
                    h_hi(b, j, 1)
                    unit_tanh(b, j, 2)
                    unit_tanh(b, j, 3)
                    h_hi(b, j, 2)
                    h_hi(b, j, 3)
                if not last:
                    q_hi(b, j)
                    v_hi(b, j)
                if behind:
                    unit_tanh(b, j, 4)
                    unit_tanh(b, j, 5)
                    h_hi(b, j, 4)
                    h_hi(b, j, 5)
                if s in turns if isinstance(s, int) else False:
                    for n in turns[s]:
                        split(n)

            def split(n):
                act.wait_ge(sem(f"w_loaded{n % 3}"), 16 * (n // 3 + 1))
                act.activation(halves(n, 0), staged(n), ACT.Copy).then_inc(sem("w_hi"), 1)

            for n in range(2):
                act.wait_ge(sem("wprod_done"), n + 1)
                act.activation((wA, wV)[n][:, 0, :, :].rearrange("p k n -> p (k n)"), banks[n][:, :], ACT.Copy
                               ).then_inc(sem("wprod_hi"), 1)
            act.wait_ge(sem("gam_done"), 1)
            x_gamma(0, -1)
            x_hi(0, -1)
            q_hi(0, -1)
            v_hi(0, -1)
            slots(act, slot)
            slot(B, 0, last=True)
            act.wait_ge(sem("vlo_done"), NP + 1)
            for n in range(N_W13, NW):
                split(n)

            def step(n, u):
                known = isinstance(n, int)
                if not known or n + 1 < NBLK:
                    wait(act, "rT_tp", n + 2)
                    wait(act, "egu_done", n)
                    v = (u + 1) % 2
                    act.activation(rT[:, v, :, :, :].rearrange("p h k n -> p (h k n)"),
                                   banks[v].bitcast(f16)[:, 0:512], ACT.Copy, scale=1.0 / UP
                                   ).then_inc(sem("rT_done"), 1)
                if not known or 0 <= n < NBLK:
                    wait(act, "egu_done", n + 1)
                    wait(act, "eh_done", n - 1)
                    act.activation(eth[:, u % 2, :], banks[2 + u % 2][:, 0:FE], ACT.Tanh, scale=0.5
                                   ).then_inc(sem("eth_done"), 1)
                if not known or 0 <= n - 1 < NBLK:
                    v = (u - 1) % 2
                    wait(act, "ehT_tp", n)
                    wait(act, "edown_done", n - 2)
                    act.activation(ehT[0:FH, v, 0, :, :].rearrange("p k n -> p (k n)"), banks[4 + v][0:FH, 0:256],
                                   ACT.Copy).then_inc(sem("ehThi_done"), 1)

            step(-1, -1)
            for n in range(RING):
                step(n, n)
            with act.Fori(1, NBLK // RING - 1) as i:
                for u in range(RING):
                    step(i * RING + u, u)
            for n in range(NBLK - RING, NBLK + 1):
                step(n, n % RING)

        @block.vector
        def _(dve):
            X16 = x_bank.bitcast(f16)
            ts, tt, stt = dve.tensor_scalar, dve.tensor_tensor, dve.scalar_tensor_tensor

            def x_stats(b, j, k=2):
                q = b * SLOTS + j + k
                par = (j + k) % 2
                loads = (b * SLOTS + (j + k) - par) * 8 + 16
                wait(dve, f"x_loaded{par}", loads)
                link, n = chained(dve, "xstat_steps", 2, q)
                dve.bn_stats(st[:, 0, :], x_in[:, par, 0, :])
                link(dve.bn_stats(st[:, 1, :], x_in[:, par, 1, :]))
                wait(dve, "xn_done", q - 1)
                dve.memset(idle_dve[:, :], 0.0)
                dve.bn_aggr(mv1[:, par, 0, :], st[:, 0, :])
                link(dve.bn_aggr(mv1[:, par, 1, :], st[:, 1, :]))
                assert n[0] == 2
                wait(dve, "xpow_done", q)
                ts(b1[:, 0, :], mv1[:, par, :, 1], EPS, None, ALU.add)
                ts(b1[:, 1, :], mv1[:, par, :, 1], (1 + EPS) / UP / UP, EPS * EPS / UP / UP, ALU.mult, ALU.add
                   ).then_inc(sem("xbase_done"), 1)

            def x_norm(b, j):
                q = b * SLOTS + j + 1
                par = (j + 1) % 2
                wait(dve, "xpow_done", q + 1)
                wait(dve, "x1_done", 2 * (q - 1))
                wait(dve, "y16lo_done", q - 1)
                wait(dve, "xT_tp", q)
                for t in range(2):
                    ts(n32[:, t, :], x_in[:, par, t, :], mv1[:, par, t, 0:1], r1[:, par, 1, t:t + 1],
                       ALU.subtract, ALU.mult)
                    ts(n16[:, 0, t, :], x_in[:, par, t, :], mv1[:, par, t, 0:1], r1[:, par, 1, t:t + 1],
                       ALU.subtract, ALU.mult)
                    ins = ts(xz[:, par, t, :], x_in[:, par, t, :], mv1[:, par, t, 0:1], r1[:, par, 0, t:t + 1],
                             ALU.subtract, ALU.mult)
                ins.then_inc(sem("xn_done"), 1)

            def x_sum(b, j):
                q = b * SLOTS + j + 1
                wait(dve, "xg_done", q + 1)
                for k in range(KD):
                    ins = stt(xg[:, k, :], X16[:, 512 + k * 256:512 + (k + 1) * 256], gam[:, 0, k:k + 1],
                              xg[:, k, :], ALU.mult, ALU.add)
                ins.then_inc(sem("xsum_done"), 1)

            def q_lo(b, j):
                q = b * SLOTS + j + 1
                wait(dve, "qhi_done", q + 1)
                flat = lambda hl: qT[:, hl, (j + 1) % 2, :, :].rearrange("p k n -> p (k n)")
                tt(flat(1), x_bank[:, :], flat(0).bitcast(f32), ALU.subtract).then_inc(sem("qlo_done"), 1)

            def v_lo(b, j):
                q = b * SLOTS + j + 1
                c = ((j + 1) % SLOTS) * 2
                wait(dve, "vhi_done", q + 1)
                flat = lambda hl: vp[:, hl, c:c + 2, :].rearrange("p k n -> p (k n)")
                tt(flat(1), x_bank[:, :], flat(0).bitcast(f32), ALU.subtract).then_inc(sem("vlo_done"), 1)

            def row_max(b, j, a):
                g = (b * SLOTS + j) * 2 + a
                n = (2 * j + a + 1) * P
                wait(dve, "qk_done", g + 1)
                dve.tensor_reduce(rmax[:, a:a + 1], scores[:, 0:n], AX.X, ALU.max).then_inc(sem("rmax_done"), 1)
                wait(dve, "rmax_done", g + 1)
                ts(nmax[:, a:a + 1], rmax[:, a:a + 1], -SCALE, math.log(UP), ALU.mult, ALU.add
                   ).then_inc(sem("nmax_done"), 1)

            def p_lo(b, j, a):
                g = (b * SLOTS + j) * 2 + a
                n = (2 * j + a + 1) * P
                wait(dve, "pexp_done", g + 1)
                tt(p16[:, 1, 0:n], p32[:, 0:n], p16[:, 0, 0:n], ALU.subtract).then_inc(sem("plo_done"), 1)

            def pT_lo(b, j, a):
                g = (b * SLOTS + j) * 2 + a
                n = 2 * j + a + 1
                wait(dve, "pT_tp", 2 * g + 2)
                wait(dve, "pv_done", g)
                dve.tensor_copy(pT[:, 1, 0:n, :].rearrange("p k q -> p (k q)"),
                                t_banks[1].bitcast(f16)[:, 0:n * P]).then_inc(sem("pTlo_done"), 1)

            def attended(b, j, a):
                s = b * SLOTS + j
                g = s * 2 + a
                par, ring = j % 2, j % 4
                dve.reciprocal(rinv[:, a:a + 1], rsum[:, a:a + 1]).then_inc(sem("rinv_done"), 1)
                wait(dve, "rinv_done", g + 1)
                wait(dve, "pv_done", g + 1)
                wait(dve, "xz_done", s + 1)
                if not isinstance(s, int):
                    dve.wait_ge(sem(f"xs_stored{par}"), (s - 4 - par) * 8 + 16)
                elif s >= 4:
                    dve.wait_ge(sem(f"xs_stored{par}"), ((s - 4) // 2 + 1) * 16)
                stt(x1[:, ring, a, :], o_bank[:, a * D:(a + 1) * D], rinv[:, a:a + 1], xz[:, par, a, :],
                    ALU.mult, ALU.add).then_inc(sem("x1_done"), 1)
                wait(dve, "x1_done", g + 1)
                dve.bn_stats(st[:, 2 + a, :], x1[:, ring, a, :]).then_inc(sem("st2_done"), 1)
                wait(dve, "st2_done", g + 1)
                dve.memset(idle_dve[:, :], 0.0)
                dve.bn_aggr(mv2[:, par, a, :], st[:, 2 + a, :]).then_inc(sem("mv2_done"), 1)
                if a == 1:
                    wait(dve, "mv2_done", g + 1)
                    wait(dve, "ypow_done", s)
                    ts(b2[:, :], mv2[:, par, :, 1], EPS, 1.0 / UP / UP, ALU.add, ALU.mult
                       ).then_inc(sem("ybase_done"), 1)

            def y_norm(b, j):
                p = b * SLOTS + j - 1
                par, ring = (j + 1) % 2, (j + 3) % 4
                wait(dve, "ypow_done", p + 1)
                wait(dve, "n16lo_done", p + 2)
                if not isinstance(p, int):
                    dve.wait_ge(sem(f"rows_stored{par}"), (p - 2 - par) * 32 + 64)
                elif p >= 2:
                    dve.wait_ge(sem(f"rows_stored{par}"), ((p - 2) // 2 + 1) * 64)
                for t in range(2):
                    args = (x1[:, ring, t, :], mv2[:, par, t, 0:1], r2[:, par, t:t + 1], ALU.subtract, ALU.mult)
                    ts(n32[:, t, :], *args)
                    ins = ts(y16[:, par, 0, t, 0:D], *args)
                ins.then_inc(sem("y16hi_done"), 1)

            def y_rows(b, j):
                p = b * SLOTS + j - 1
                par = (j + 1) % 2
                wait(dve, "y16lo_done", p + 1)
                dve.tensor_copy(y16[:, par, 1, :, 0:2 * D], y16[:, par, 0, :, 0:2 * D])
                ids = y16[:, par, :, :, :].bitcast(i32)[:, :, :, D]
                dve.tensor_copy(ids, idtab[:, ds(p, 1), :, :].rearrange("p a k t -> p (a k) t")
                                ).then_inc(sem("rows_ready"), 1)

            def shared_sum(b, j, t):
                p = b * SLOTS + j - 2
                wait(dve, "down_done", 2 * p + t + 1)
                row = x1[:, (j + 2) % 4, t, :]
                stt(row, t_banks[t][:, 0:D], sg[:, j % 2, t:t + 1], row, ALU.mult, ALU.add
                    ).then_inc(sem("xs_done"), 1)

            ROUTE = 18

            def route_a(b, j):
                p = b * SLOTS + j - 1
                wait(dve, "logits_done", p + 1)
                wait(dve, "mask_done", p)
                dve.tensor_copy(lg[:, :, :], s_banks[0][:, 0:20].rearrange("p (t n) -> p t n", t=2)
                                ).then_inc(sem("logits_read"), 1)
                wait(dve, "logits_read", p + 1)
                link, c = chained(dve, "ra_steps", 1, p)
                link(dve.tensor_reduce(small[:, 0, :], lg[:, :, 0:NE], AX.X, ALU.max))
                tt(sh[:, :, :], lg[:, :, 0:NE], bc(small[:, 0, :], NE), ALU.subtract
                   ).then_inc(sem("shifted_done"), 1)

            def route_b(b, j):
                p = b * SLOTS + j - 1
                par = (j + 1) % 2
                wait(dve, "rexp_done", p + 1)
                wait(dve, "prefix_done", p)
                link, c = chained(dve, "rb_steps", ROUTE, p)
                link(dve.tensor_reduce(small[:, 1, :], ex[:, :, :], AX.X, ALU.add))
                link(dve.reciprocal(small[:, 2, :], small[:, 1, :]))
                link(tt(pr[:, :, :], ex[:, :, :], bc(small[:, 2, :], NE), ALU.mult))
                for k in range(2):
                    v = vtmp[:, k, :]
                    link(dve.tensor_reduce(v, pr[:, :, :], AX.X, ALU.max))
                    link(tt(ca[:, :, :], pr[:, :, :], bc(v, NE), ALU.is_equal))
                    link(tt(cb[:, :, :], ca[:, :, :], w8[:, :, :], ALU.mult))
                    link(dve.tensor_reduce(small[:, 3, :], cb[:, :, :], AX.X, ALU.max))
                    link(tt(one[:, k, :, :], cb[:, :, :], bc(small[:, 3, :], NE), ALU.is_equal))
                    if k == 0:
                        link(stt(pr[:, :, :], one[:, 0, :, :], -2.0, pr[:, :, :], ALU.mult, ALU.add))
                dve.tensor_copy(wts[:, ds(p, 1), :, :].rearrange("p a k t -> p (a k) t"), vtmp[:, :, :])
                link(ts(sg[:, par, :], tg[:, :], 1.0, 0.5, ALU.add, ALU.mult))
                link(tt(mk[:, :, :], one[:, 0, :, :], one[:, 1, :, :], ALU.add))
                link(dve.tensor_copy(cum[:, par, 0, :], cum[:, 1 - par, 2, :]))
                link(tt(cum[:, par, 1, :], cum[:, par, 0, :], mk[:, 0, :], ALU.add))
                tt(cum[:, par, 2, :], cum[:, par, 1, :], mk[:, 1, :], ALU.add).then_inc(sem("mask_done"), 1)
                assert c[0] == ROUTE, c[0]

            def route_c(b, j):
                p = b * SLOTS + j - 1
                par = (j + 1) % 2
                wait(dve, "prefix_done", p + 1)
                tt(dd[:, :, :], s_banks[0][:, 0:2 * NE].rearrange("p (t e) -> p t e", t=2), eoff[:, :, :], ALU.add
                   ).then_inc(sem("prefix_read"), 1)
                wait(dve, "prefix_read", p + 1)
                link, c = chained(dve, "rc_steps", 2, p)
                tt(ca[:, :, :], dd[:, :, :], one[:, 0, :, :], ALU.mult)
                link(tt(cb[:, :, :], dd[:, :, :], one[:, 1, :, :], ALU.mult))
                dve.tensor_reduce(df[:, 0, :], ca[:, :, :], AX.X, ALU.add)
                link(dve.tensor_reduce(df[:, 1, :], cb[:, :, :], AX.X, ALU.add))
                dve.tensor_copy(di[:, par, :, :], df[:, :, :]).then_inc(sem("dest_done"), 1)
                assert c[0] == 2

            def unit_h(b, j, u):
                p = b * SLOTS + j - 1
                g = g_banks[u % 2]
                m = 64 if u == UNITS - 1 else P
                wait(dve, "th_done", UNITS * p + u + 1)
                wait(dve, "hlo_done", (UNITS - 1) * p + max(u - 1, 0))
                wait(dve, "hhi_done", UNITS * p + u - 1)
                up = g[64:P, 0:256] if u == UNITS - 1 else g[:, 256:512]
                a = th[64:P, 1, :] if u == UNITS - 1 else th[:, u % 2, :]
                stt(a, th[0:m, u % 2, :], 1.0, g[0:m, 0:256], ALU.add, ALU.mult).then_inc(sem("ha_done"), 1)
                wait(dve, "ha_done", UNITS * p + u + 1)
                stt(h32[P - m:P, u % 2, :], a, 0.5, up, ALU.mult, ALU.mult).then_inc(sem("h_done"), 1)

            def last_lo(b, j):
                p = b * SLOTS + j - 1
                wait(dve, "hhi_done", UNITS * (p + 1))
                u = UNITS - 1
                tt(hT[64:P, 1, u, :], h32[64:P, u % 2, :], hT[64:P, 0, u, :].bitcast(f32), ALU.subtract
                   ).then_inc(sem("hlast_done"), 1)

            def split(n):
                dve.wait_ge(sem("w_hi"), n + 1)
                tt(halves(n, 1), staged(n), halves(n, 0).bitcast(f32), ALU.subtract).then_inc(sem("w_split"), 1)

            def slot(b, j, last=False):
                s = b * SLOTS + j
                known = isinstance(s, int)
                behind, behind2 = not known or s >= 1, not known or s >= 2
                if not last:
                    row_max(b, j, 0)
                if behind:
                    y_norm(b, j)
                if behind2:
                    shared_sum(b, j, 0)
                    shared_sum(b, j, 1)
                if not last:
                    p_lo(b, j, 0)
                    x_norm(b, j)
                    pT_lo(b, j, 0)
                if behind:
                    route_a(b, j)
                if not last:
                    attended(b, j, 0)
                    row_max(b, j, 1)
                if behind:
                    y_rows(b, j)
                    route_b(b, j)
                if not last:
                    p_lo(b, j, 1)
                    x_sum(b, j)
                if behind:
                    unit_h(b, j, 0)
                    unit_h(b, j, 1)
                if not last:
                    pT_lo(b, j, 1)
                if behind:
                    route_c(b, j)
                    unit_h(b, j, 2)
                    unit_h(b, j, 3)
                if not last:
                    q_lo(b, j)
                    attended(b, j, 1)
                    v_lo(b, j)
                if behind:
                    unit_h(b, j, 4)
                    unit_h(b, j, 5)
                if not last:
                    x_stats(b, j)
                if behind:
                    last_lo(b, j)
                if s in turns if isinstance(s, int) else False:
                    for n in turns[s]:
                        split(n)

            dve.memset(half[:, :], -0.5)
            dve.memset(ones[:, :], 1.0)
            dve.memset(cum[:, :, :, :], 0.0).then_inc(sem("dconst_done"), 1)
            x_stats(0, -2)
            dve.wait_ge(sem("gam_loaded"), 32)
            ts(gam[:, 0, :], gam_in[:, 0, :], 1.0 / UP, None, ALU.mult)
            dve.tensor_copy(gam[:, 1, :], gam_in[:, 1, :])
            dve.tensor_copy(wR[:, 0, :, :], r_in[:, :, :]).then_inc(sem("gam_done"), 1)
            dve.wait_ge(sem("gam_done"), 1)
            tt(wR[:, 1, :, :], r_in[:, :, :], wR[:, 0, :, :].bitcast(f32), ALU.subtract)
            x_norm(0, -1)
            dve.wait_ge(sem("consts_built"), 3)
            dve.tensor_copy(ident16[:, :], identf[:, :])
            dve.tensor_copy(identr[:, :], identf[:, :])
            dve.tensor_copy(mask[:, :, :], maskf[:, :, :])
            dve.tensor_copy(upper[:, :], upf[:, :]).then_inc(sem("consts_done"), 1)
            for n in range(2):
                dve.wait_ge(sem("wprod_hi"), n + 1)
                w = (wA, wV)[n]
                flat = lambda hl: w[:, hl, :, :].rearrange("p k n -> p (k n)")
                tt(flat(1), banks[n][:, :], flat(0).bitcast(f32), ALU.subtract).then_inc(sem("wprod_split"), 1)
            x_sum(0, -1)
            q_lo(0, -1)
            v_lo(0, -1)
            x_stats(0, -1)
            dve.wait_ge(sem("tables_built"), 1)
            slots(dve, slot)
            slot(B, 0, last=True)
            link, c = chained(dve, "tab_steps", 0, 0)
            dve.wait_ge(sem("count_done"), 1)
            cnt, nb, cb_, base_ = tc[:, 0, :], tc[:, 1, :], tc[:, 2, :], tc[:, 3, :]
            dve.wait_ge(sem("xz_done"), NP + 1)
            link(dve.tensor_copy(cnt, s_banks[0][:, 0:NE]))
            link(ts(tc[:, 4, :], cnt, float(P - 1), None, ALU.add))
            link(dve.tensor_copy(tci[:, :], tc[:, 4, :]))
            link(ts(tci[:, :], tci[:, :], 7, None, ALU.logical_shift_right))
            link(dve.tensor_copy(nb, tci[:, :]))
            src = nb
            for i, step_ in enumerate((1, 2, 4)):
                dst = tc[:, 5 + i, :]
                dve.tensor_copy(dst[:, 0:step_], src[:, 0:step_])
                link(tt(dst[:, step_:NE], src[:, step_:NE], src[:, 0:NE - step_], ALU.add))
                src = dst
            link(tt(tc[:, 8, :], cnt, eoff[:, 0, :], ALU.add))
            dve.tensor_copy(pad_i[0:1, :], tc[0:1, 8, :]).then_inc(sem("pad_ready"), 1)
            link(ts(tc[:, 9, :], nb, -float(P), float(ROWS), ALU.mult, ALU.add))
            blk_b = blk[0:1, :].rearrange("p (n o) -> p n o", o=1).to_broadcast([1, NBLK, NE])
            ends_b = src[0:1, :].rearrange("p (o e) -> p o e", o=1).to_broadcast([1, NBLK, NE])
            gain_b = tc[0:1, 9, :].rearrange("p (o e) -> p o e", o=1).to_broadcast([1, NBLK, NE])
            link(tt(tb[:, :, :], blk_b, ends_b, ALU.is_ge))
            link(dve.tensor_reduce(tw[:, 0, :], tb[:, :, 0:NE - 1], AX.X, ALU.add))
            link(tt(tbb[:, :, :], tb[:, :, :], gain_b, ALU.mult))
            link(dve.tensor_reduce(tw[:, 1, :], tbb[:, :, 0:NE - 1], AX.X, ALU.add))
            link(ts(tc[:, 10, :], src, -float(P), float(NE * ROWS), ALU.mult, ALU.add))
            link(stt(tw[:, 2, :], tw[:, 1, :], tc[0:1, 10, NE - 1:NE], tb[:, :, NE - 1], ALU.subtract, ALU.mult))
            link(tt(tw[:, 1, :], tw[:, 1, :], tw[:, 2, :], ALU.subtract))
            link(stt(tw[:, 1, :], blk[:, :], float(P), tw[:, 1, :], ALU.mult, ALU.add))
            dve.tensor_copy(tab_e[:, :], tw[:, 0, :])
            dve.tensor_copy(tab_r[:, :], tw[:, 1, :]).then_inc(sem("table_done"), 1)
            shared_sum(B, 1, 0)
            shared_sum(B, 1, 1)
            for n in range(N_W13, NW):
                split(n)

            def step(n, u):
                known = isinstance(n, int)
                if not known or 0 <= n < NBLK:
                    wait(dve, "eth_done", n + 1)
                    g = banks[2 + u % 2]
                    wait(dve, "ehT_tp", n - 1)
                    stt(eth[:, u % 2, :], eth[:, u % 2, :], 1.0, g[:, 0:FE], ALU.add, ALU.mult
                        ).then_inc(sem("ea_done"), 1)
                    wait(dve, "ea_done", n + 1)
                    stt(eh[:, u % 2, :], eth[:, u % 2, :], 0.5, g[:, FE:2 * FE], ALU.mult, ALU.mult
                        ).then_inc(sem("eh_done"), 1)
                if not known or 0 <= n - 1 < NBLK:
                    v = (u - 1) % 2
                    wait(dve, "ehThi_done", n)
                    flat = lambda hl: ehT[0:FH, v, hl, :, :].rearrange("p k n -> p (k n)")
                    tt(flat(1), banks[4 + v][0:FH, 0:256], flat(0).bitcast(f32), ALU.subtract
                       ).then_inc(sem("ehT_done"), 1)
                if not known or 0 <= n - 2 < NBLK:
                    r = (u - 2) % RING
                    wait(dve, "edown_done", n - 1)
                    if known:
                        wait(dve, f"scattered{r}", ((n - 2) // RING) * 16)
                    else:
                        dve.wait_ge(sem(f"scattered{r}"), (n - 2 - r) * 2)
                    dve.tensor_copy(eo[:, r, :], banks[6 + r % 2][:, 0:D]).then_inc(sem("eo_done"), 1)

            dve.wait_ge(sem("xs_done"), 2 * NP)
            for par in (0, 1):
                dve.wait_ge(sem(f"xs_stored{par}"), 16 * (NP // 2))
            for n in range(RING):
                step(n, n)
            with dve.Fori(1, NBLK // RING - 1) as i:
                for u in range(RING):
                    step(i * RING + u, u)
            for n in range(NBLK - RING, NBLK + 2):
                step(n, n % RING)

            def combine(pair, u, i):
                dve.wait_ge(sem(f"parts_loaded{u}"), i * 48 + 48)
                for k in range(2):
                    for t in range(2):
                        row = cx[:, u, 0, t, :]
                        w = wts[:, ds(pair, 1), k, t:t + 1].rearrange("p a t -> p (a t)")
                        ins = stt(row, cx[:, u, 1 + k, t, :], w, row, ALU.mult, ALU.add)
                    ins.then_inc(sem("combine_half" if k == 0 else "combined"), 1)
                    if k == 0:
                        dve.wait_ge(sem("combine_half"), pair + 1)

            with dve.Fori(0, NP // PARTS) as i:
                for u in range(PARTS):
                    combine(i * PARTS + u, u, i)

        @block.gpsimd
        def _(pool):
            def x_pow(b, j, k):
                q = b * SLOTS + j + k
                par = (j + k) % 2
                wait(pool, "xbase_done", q + 1)
                wait(pool, "xn_done", q - 1)
                pool.tensor_tensor(r1[:, par, :, :], b1[:, :, :],
                                   half[:, :].rearrange("p (a t) -> p a t", a=2), ALU.pow
                                   ).then_inc(sem("xpow_done"), 1)

            def x_pool(b, j):
                q = b * SLOTS + j + 1
                par = (j + 1) % 2
                wait(pool, "xn_done", q + 1)
                pool.tensor_tensor(n16[:, 1, :, :], n32[:, :, :], n16[:, 0, :, :], ALU.subtract
                                   ).then_inc(sem("n16lo_done"), 1)
                pool.tensor_tensor(xz[:, par, :, :], xz[:, par, :, :], x_in[:, par, :, :], ALU.add
                                   ).then_inc(sem("xz_done"), 1)

            def x_lo(b, j):
                q = b * SLOTS + j + 1
                c = ((j + 1) % SLOTS) * 2 * P
                wait(pool, "xhi_done", q + 1)
                pool.tensor_tensor(xT[:, 1, :, c:c + 2 * P], xg[:, :, :], xT[:, 0, :, c:c + 2 * P].bitcast(f32),
                                   ALU.subtract).then_inc(sem("xlo_done"), 1)

            def y_pow(b, j):
                p = b * SLOTS + j - 1
                par = (j + 1) % 2
                wait(pool, "ybase_done", p + 1)
                pool.tensor_tensor(r2[:, par, :], b2[:, :], half[:, 0:2], ALU.pow).then_inc(sem("ypow_done"), 1)

            def y_lo(b, j):
                p = b * SLOTS + j - 1
                par = (j + 1) % 2
                wait(pool, "y16hi_done", p + 1)
                pool.tensor_tensor(y16[:, par, 0, :, D:2 * D], n32[:, :, :], y16[:, par, 0, :, 0:D], ALU.subtract
                                   ).then_inc(sem("y16lo_done"), 1)

            def h_lo(b, j, u):
                p = b * SLOTS + j - 1
                if u == UNITS - 2:
                    wait(pool, "dest_done", p + 1)
                    wait(pool, "rows_ready", p + 1)
                wait(pool, "hhi_done", UNITS * p + u + 1)
                pool.tensor_tensor(hT[:, 1, u, :], h32[:, u % 2, :], hT[:, 0, u, :].bitcast(f32),
                                   ALU.subtract).then_inc(sem("hlo_done"), 1)

            def scatter(b, j):
                p = b * SLOTS + j - 1
                par = (j + 1) % 2
                for k in range(2):
                    for t in range(2):
                        pool.indirect_dma_start(
                            out=row_tab, out_offset=bass.IndirectOffsetOnAxis(ap=di[:, par, k, t:t + 1], axis=0),
                            in_=y16[:, par, k, t, :], in_offset=None
                        ).then_inc(sem(f"rows_stored{par}"), 16)

            def slot(b, j, last=False):
                s = b * SLOTS + j
                behind = not isinstance(s, int) or s >= 1
                if behind:
                    y_pow(b, j)
                    y_lo(b, j)
                if not last:
                    x_pow(b, j, 1)
                    x_pool(b, j)
                if behind:
                    h_lo(b, j, 0)
                if not last:
                    x_lo(b, j)
                if behind:
                    for u in range(1, UNITS - 1):
                        h_lo(b, j, u)
                    scatter(b, j)

            pool.memset(identf[:, :], 0.0)
            pool.memset(maskf[:, :, :], 0.0)
            pool.memset(upf[:, :], 1.0)
            pool.memset(idle[:, :], 0.0).then_inc(sem("pconst"), 1)
            pool.wait_ge(sem("pconst"), 1)
            pool.affine_select(out=identf[:, :], in_=identf[:, :], compare_op=ALU.not_equal, fill=1.0, base=0,
                               pattern=[[-1, P]], channel_multiplier=1).then_inc(sem("consts_built"), 1)
            for a in range(2):
                pool.affine_select(out=maskf[:, a, a * P:(a + 1) * P], in_=maskf[:, a, a * P:(a + 1) * P],
                                   compare_op=ALU.is_ge, fill=MASKED, base=0, pattern=[[-1, P]],
                                   channel_multiplier=1)
            pool.affine_select(out=upf[:, :], in_=upf[:, :], compare_op=ALU.is_gt, fill=0.0, base=0,
                               pattern=[[1, P]], channel_multiplier=-1).then_inc(sem("consts_built"), 2)
            pool.wait_ge(sem("dconst_done"), 1)
            x_pow(0, -1, 1)
            x_pool(0, -1)
            pool.iota(idtab[:, :, :, :], [[2 * P, NP], [T, 2], [P, 2]], base=0, channel_multiplier=1)
            pool.iota(w8[:, :, :], [[0, 2], [-1, NE]], base=NE, channel_multiplier=0,
                      allow_small_or_imprecise_dtypes=True)
            pool.iota(eoff[:, :, :], [[0, 2], [ROWS, NE]], base=0, channel_multiplier=0,
                      allow_small_or_imprecise_dtypes=True)
            pool.iota(blk[:, :], [[1, NBLK]], base=0, channel_multiplier=0, allow_small_or_imprecise_dtypes=True
                      ).then_inc(sem("tables_built"), 1)
            x_lo(0, -1)
            slots(pool, slot)
            slot(B, 0, last=True)

            pool.wait_ge(sem("vlo_done"), NP + 1)
            pool.memset(pad_rows[:, :], 0.0)
            pool.iota(pad_ids[:, :], [[P, SPARE]], base=2 * T, channel_multiplier=1
                      ).then_inc(sem("pad_rows_built"), 1)

            def scatter_block(n, u):
                wait(pool, "eo_done", n + 1)
                wait(pool, "idle_done", n)
                pool.tensor_tensor(idle[:, :], half[:, 0:2], half[:, 0:2], ALU.add).then_inc(sem("idle_done"), 1)
                pool.indirect_dma_start(
                    out=exp_tab,
                    out_offset=bass.IndirectOffsetOnAxis(ap=rows[:, u, :].bitcast(i32)[:, D:D + 1], axis=0),
                    in_=eo[:, u, :], in_offset=None).then_inc(sem(f"scattered{u}"), 16)

            for u in range(RING):
                scatter_block(u, u)
            with pool.Fori(1, NBLK // RING) as i:
                for u in range(RING):
                    scatter_block(i * RING + u, u)
            for u in range(RING):
                pool.wait_ge(sem(f"scattered{u}"), 16 * (NBLK // RING))


def kernel(**inputs):
    import numpy as np
    import concourse.bacc as bacc
    from concourse.bass_utils import run_bass_kernel_spmd

    a = {k.removeprefix("L0_"): np.asarray(v) for k, v in inputs.items()}
    flat = np.ascontiguousarray
    qkv = a["attn_qkv"]
    gu = a["ffn_shared_gate_up_w"].T
    order = np.concatenate([np.arange(o + u * P, min(o + (u + 1) * P, o + F))
                            for u in range(UNITS) for o in (0, F)])
    router = np.zeros((D, 10), np.float32)
    router[:, 0:NE] = a["ffn_gate_w"].T
    router[:, NE:NE + 1] = a["ffn_shared_gate_w"].T
    arrays = {
        "x": a["attn_x"].reshape(T, D), "wqT": flat(qkv[:, 0:D].T), "wkT": flat(qkv[:, D:2 * D].T),
        "wvT": flat(qkv[:, 2 * D:].T), "wo": a["attn_o_proj"], 
        "gamma_beta": flat(np.stack([a["attn_gamma"], a["attn_beta"]]).reshape(2, KD, P).transpose(2, 0, 1)),
        "router": router, "wgu": flat(gu[:, order]), "wsd": flat(a["ffn_shared_down_w"].T),
        "w13": flat(a["ffn_w13"].transpose(0, 2, 1)), "w2": flat(a["ffn_w2"].transpose(0, 2, 1)),
    }
    nc = bacc.Bacc("TRN2", target_bir_lowering=False, num_devices=1)
    args = [nc.dram_tensor(n, v.shape, mybir.dt.from_np(v.dtype), kind="ExternalInput").ap()
            for n, v in arrays.items()]
    out = nc.dram_tensor("out", (T, D), mybir.dt.float32, kind="ExternalOutput").ap()
    program(nc, *args, out)
    r = run_bass_kernel_spmd(nc, [arrays], core_ids=[0])
    return r.results[0]["out"].reshape(B, S, D)
```

```python
import math

import concourse.bass as bass
from concourse import mybir

B, S, D = 4, 1024, 256
T = B * S
P = 128
NP = T // (2 * P)
SLOTS = S // (2 * P)
KD = D // P
F = 704
UNITS = 6
NE = 8
FE = 176
FH = FE // 2
ROWS = T + P
RW = 2 * D + 2
SPARE = 2 * NE
NBLK = (2 * T + NE * (P - 1)) // P + 1
RING = 8
PARTS = 4
EPS = 1e-5
SCALE = 1.0 / math.sqrt(D)
UP = 1024.0
MASKED = -1e30
MADE_ON_CHIP = "the chip has worked it out from counts that add up to 2 T"


def program(nc, x, wqT, wkT, wvT, wo, gamma_beta, router, wgu, wsd, w13, w2, out):
    dt = mybir.dt
    f32, f32r, f16, bf16, i32 = dt.float32, dt.float32r, dt.float16, dt.bfloat16, dt.int32
    ALU, ACT, AX = mybir.AluOpType, mybir.ActivationFunctionType, mybir.AxisListType
    ds = bass.ds

    row_tab = nc.dram_tensor("row_tab", ((NE * ROWS + (SPARE - NE) * P), RW), f16, kind="Internal").ap()
    exp_tab = nc.dram_tensor("exp_tab", (2 * T + SPARE * P, D), f32, kind="Internal").ap()
    pad_tab = nc.dram_tensor("pad_tab", (NE * P, RW), f16, kind="Internal").ap()
    xs_tab = nc.dram_tensor("xs_tab", (T, D), f32, kind="Internal").ap()

    top = [-(-nc.sbuf_base // 64) * 64]
    size = {f32: 4, f32r: 4, f16: 2, bf16: 2, i32: 4}

    def place(name, shape, dtype, at=None):
        n = size[dtype]
        for d in shape[1:]:
            n *= d
        where = top[0] if at is None else at
        if at is None:
            top[0] += -(-n // 32) * 32
        return nc.alloc_sbuf_tensor_at(name, shape, dtype, offset=where)

    base_kv = top[0]
    xT = place("xT", [P, 2, KD, S], f32r)
    vp = place("vp", [P, 2, 2 * SLOTS, D], f32r)
    base_att = top[0]
    qT = place("qT", [P, 2, 2, KD, 2 * P], f32r)
    p32 = place("p32", [P, S], f32)
    pT = place("pT", [P, 2, 2 * SLOTS, P], f32r)
    base_ffn = top[0]
    yT = place("yT", [P, 2, KD, 2 * P], f32r)
    hT = place("hT", [P, 2, UNITS, 2 * P], f32r)
    x_in = place("x_in", [P, 2, 2, D], f32)
    xz = place("xz", [P, 2, 2, D], f32)
    base_x1 = top[0]
    x1 = place("x1", [P, 4, 2, D], f32)
    nx = place("nx", [P, 2, D], f32)
    ny = place("ny", [P, 2, D], f32)
    y16 = place("y16", [P, 2, 2, 2, RW], f16)
    xg = place("xg", [P, KD, 2 * P], f32)
    th = place("th", [P, 2, 2 * P], f32)
    h32 = place("h32", [P, 2, 2 * P], f32)
    stage = place("stage", [P, 3, F], f32)
    wA = place("wA", [P, 2, KD, D], f32r)
    wV = place("wV", [P, 2, KD, D], f32r)
    wR = place("wR", [P, KD, 2, 10], f32r)
    base_wG = top[0]
    wG = place("wG", [P, 2, KD, 2 * F], f32r)
    wS = place("wS", [P, 2, UNITS, D], f32r)
    wE = place("wE", [P, 2, NE, KD, 2 * FE], f32r)
    ident16 = place("ident16", [P, P], f16)
    identf = place("identf", [P, P], f32)
    identr = place("identr", [P, P], f32r)
    mask = place("mask", [P, 2, 2 * P], f32r)
    upper = place("upper", [P, P], bf16)
    ones = place("ones", [P, P], bf16)
    idtab = place("idtab", [P, NP, 2, 2], i32)
    wts = place("wts", [P, NP, 2, 2], f32)
    w8 = place("w8", [P, 2, NE], f32)
    eoff = place("eoff", [P, 2, NE], f32)
    gam = place("gam", [P, 2, KD], f32)
    half = place("half", [P, 4], f32)
    st = place("st", [P, 4, 6], f32)
    mv1 = place("mv1", [P, 2, 2, 2], f32)
    mv2 = place("mv2", [P, 2, 2, 2], f32)
    b1 = place("b1", [P, 2, 2], f32)
    r1 = place("r1", [P, 2, 2, 2], f32)
    b2 = place("b2", [P, 2], f32)
    r2 = place("r2", [P, 2, 2], f32)
    rmax = place("rmax", [P, 2], f32)
    nmax = place("nmax", [P, 2], f32)
    rsum = place("rsum", [P, 2], f32)
    idle = place("idle", [P, 2], f32)
    idle_dve = place("idle_dve", [P, 1], f32)
    gam_in = place("gam_in", [P, 2, KD], f32)
    r_in = place("r_in", [P, KD, 10], f32)
    rinv = place("rinv", [P, 2], f32)
    ratio = place("ratio", [P, 2, 2], f32)
    lg = place("lg", [P, 2, 10], f32)
    sh = place("sh", [P, 2, NE], f32)
    ex = place("ex", [P, 2, NE], f32)
    pr = place("pr", [P, 2, NE], f32)
    ca = place("ca", [P, 2, NE], f32)
    cb = place("cb", [P, 2, NE], f32)
    one = place("one", [P, 2, 2, NE], f32)
    small = place("small", [P, 8, 2], f32)
    vtmp = place("vtmp", [P, 2, 2], f32)
    tg = place("tg", [P, 2], f32)
    sg = place("sg", [P, 2, 2], f32)
    mk = place("mk", [P, 2, NE], bf16)
    cum = place("cum", [P, 2, 3, NE], bf16)
    dd = place("dd", [P, 2, NE], f32)
    df = place("df", [P, 2, 2], f32)
    di = place("di", [P, 2, 2, 2], i32)
    tc = place("tc", [P, 12, NE], f32)
    tci = place("tci", [P, NE], i32)
    blk = place("blk", [1, NBLK], f32)
    tab_e = place("tab_e", [1, NBLK], i32)
    tab_r = place("tab_r", [1, NBLK], i32)
    pad_i = place("pad_i", [1, NE], i32)
    assert top[0] <= nc.sbuf_usable_end, (top[0], nc.sbuf_usable_end)
    base_h = base_ffn + 2 * KD * 2 * P * 4
    w_raw = [place(f"w_raw{i}", [P, KD, D], f32, at=base_h + i * KD * D * 4) for i in range(4)]
    maskf = place("maskf", [P, 2, 2 * P], f32, at=base_att + 8192)
    upf = place("upf", [P, P], f32, at=base_att + 8192 + 4 * 512)
    w2s = place("w2s", [P, 2, NE, 2, D], f32r, at=base_kv)
    at = [base_att]

    def later(name, shape, dtype, room):
        n = size[dtype]
        for d in shape[1:]:
            n *= d
        t = place(name, shape, dtype, at=at[0])
        at[0] += -(-n // 32) * 32
        assert at[0] <= room
        return t

    rows = later("rows", [P, RING, RW], f16, base_ffn)
    rT = later("rT", [P, 2, 2, KD, P], f32r, base_ffn)
    eth = later("eth", [P, 2, FE], f32, base_ffn)
    eh = later("eh", [P, 2, FE], f32, base_ffn)
    ehT = later("ehT", [P, 2, 2, 2, P], f32r, base_ffn)
    eo = place("eo", [P, RING, D], f32, at=base_x1)
    at = [base_ffn + 16384]
    tb = later("tb", [1, NBLK, NE], f32, base_ffn + 24576)
    tbb = later("tbb", [1, NBLK, NE], f32, base_ffn + 24576)
    tw = later("tw", [1, 4, NBLK], f32, base_ffn + 24576)
    at = [base_ffn]
    cx = later("cx", [P, PARTS, 2, 2, D], f32, base_ffn + 24576)
    acc = place("acc", [P, NP, 2, D], f32, at=base_wG)

    scores = nc.alloc_psum_tensor("scores", [P, 2 * 512], f32)
    probsT = nc.alloc_psum_tensor("probsT", [P, 2 * 512], f32)
    banks = [t[:, c:c + 512] for t in (scores, probsT) for c in (0, 512)]
    banks += [nc.alloc_psum_tensor(f"bank{i}", [P, 512], f32)[:, :] for i in range(4, 8)]
    s_banks, t_banks, g_banks = banks[0:2], banks[2:4], banks[5:7]
    o_bank, x_bank = banks[4], banks[7]

    pads = y16[:, :, :, :, :].rearrange("p a k t w -> p (a k t) w")

    sems = {}

    def sem(name):
        if name not in sems:
            sems[name] = nc.alloc_semaphore(name)
        return sems[name]

    def wait(e, name, n):
        if isinstance(n, int) and n <= 0:
            return
        e.wait_ge(sem(name), n)

    def chained(e, name, per, n):
        count = [0]

        def link(ins):
            count[0] += 1
            ins.then_inc(sem(name), 1)
            wait(e, name, n * per + count[0])
        return link, count

    def bc(ap, n):
        return ap.rearrange("p (a o) -> p a o", o=1).to_broadcast([P, ap.shape[1], n])

    def products(pe, dst, lhs, rhs, first=True, last=True):
        for n, (a, b) in enumerate(((0, 0), (0, 1), (1, 0))):
            ins = pe.matmul(dst, lhs(a), rhs(b), start=first and n == 0, stop=last and n == 2)
        return ins

    def chunks_of(j, a):
        n = 2 * j + a + 1
        return [(c, min(c + 4, n)) for c in range(0, n, 4)]

    def chunks_before(b, j, a):
        before = sum(len(chunks_of(j_, a_)) for j_ in range(j) for a_ in range(2))
        whole = sum(len(chunks_of(j_, a_)) for j_ in range(SLOTS) for a_ in range(2))
        return b * whole + before + a * len(chunks_of(j, 0))

    def down_out(j, t):
        return t_banks[1][:, t * D:(t + 1) * D] if j < 2 else t_banks[t][:, 0:D]

    def slots(e, slot):
        for j in range(SLOTS):
            slot(0, j)
        with e.Fori(1, B) as b:
            for j in range(SLOTS):
                slot(b, j)

    chunks = []
    for k in range(KD):
        for c in (0, F):
            chunks.append((wgu[k * P:(k + 1) * P, c:c + F], lambda hl, k=k, c=c: wG[:, hl, k, c:c + F], F, 0, F))
    for k, n in ((0, 2), (2, 2), (4, 1)):
        chunks.append((wsd[k * P:(k + n) * P, :], lambda hl, k=k, n=n: wS[:, hl, k:k + n, :], n * D, 0, D))
    chunks.append((wsd[5 * P:F, :], lambda hl: wS[64:P, hl, 5:6, :], D, 64, D))
    N_FFN = len(chunks)
    for i in range(NE):
        chunks.append((w13[i], lambda hl, i=i: wE[:, hl, i, :, :], 2 * 2 * FE, 0, 2 * FE))
    N_W13 = len(chunks)
    for i in range(NE):
        chunks.append((w2[i], lambda hl, i=i: w2s[0:FH, hl, i, :, :], 2 * D, 0, D))
    NW = len(chunks)

    def staged(n):
        src, dst, width, p0, inner = chunks[n]
        rows_ = dst(0).shape[0]
        return stage[p0:p0 + rows_, n % 3, 0:width].rearrange("p (k n) -> p k n", n=inner)

    def halves(n, hl):
        dst = chunks[n][1](hl)
        return dst.rearrange("p (k n) -> p k n", k=1) if len(dst.shape) == 2 else dst

    turns = {0: range(0, N_FFN), 1: range(N_FFN, N_FFN + 3), 2: range(N_FFN + 3, N_FFN + 6),
             3: range(N_FFN + 6, N_W13)}

    with nc.Block() as block:

        @block.sync
        def _(sp):
            def first_row(pair):
                return pair * 2 * P if isinstance(pair, int) else sp.snap(pair * 2 * P)

            def load_x(pair, par, *waits):
                row = first_row(pair)
                for w in waits:
                    wait(sp, *w)
                sp.dma_start(x_in[:, par, :, :],
                             x[ds(row, 2 * P), :].rearrange("(t p) d -> p t d", p=P)
                             ).then_inc(sem(f"x_loaded{par}"), 16)

            load_x(0, 0)
            sp.dma_start(w_raw[0][:, :, :], wqT.rearrange("(k p) n -> p k n", p=P)).then_inc(sem("qkv_loaded"), 16)
            sp.dma_start(w_raw[1][:, :, :], wkT.rearrange("(k p) n -> p k n", p=P)).then_inc(sem("qkv_loaded"), 16)
            sp.dma_start(w_raw[2][:, :, :], wvT.rearrange("(k p) n -> p k n", p=P)).then_inc(sem("qkv_loaded"), 16)
            sp.dma_start(w_raw[3][:, :, :], wo.rearrange("(k p) n -> p k n", p=P)).then_inc(sem("qkv_loaded"), 16)
            sp.dma_start(gam_in[:, :, :], gamma_beta).then_inc(sem("gam_loaded"), 16)
            sp.dma_start(r_in[:, :, :], router.rearrange("(k p) n -> p k n", p=P)).then_inc(sem("gam_loaded"), 16)
            load_x(1, 1)
            def load_chunk(n):
                wait(sp, "w_split", n - 2)
                rows_ = staged(n).shape[0]
                sp.dma_start(staged(n), chunks[n][0].rearrange("(k p) n -> p k n", p=rows_)
                             ).then_inc(sem(f"w_loaded{n % 3}"), 16)

            for n in range(3):
                load_chunk(n)
            chunk = [3]

            def slot(b, j):
                s = b * SLOTS + j
                load_x((s + 2) % NP, j % 2, ("xz_done", s + 1))
                if not isinstance(s, int) or s >= 2:
                    store_xs(b, j)
                if s in turns if isinstance(s, int) else False:
                    while chunk[0] < min(turns[s].stop + 3, N_W13):
                        load_chunk(chunk[0])
                        chunk[0] += 1

            def store_xs(b, j):
                p2 = b * SLOTS + j - 2
                row = first_row(p2)
                wait(sp, "xs_done", 2 * p2 + 2)
                sp.dma_start(xs_tab[ds(row, 2 * P), :].rearrange("(t p) d -> p t d", p=P),
                             x1[:, (j + 2) % 4, :, :]).then_inc(sem(f"xs_stored{j % 2}"), 16)

            for n, dst in enumerate((pad_tab, row_tab[NE * ROWS:, :])):
                sp.wait_ge(sem("pads_built"), n + 1)
                sp.dma_start(dst.rearrange("(n p) w -> p n w", p=P), pads).then_inc(sem("pads_stored"), 16)

            slots(sp, slot)
            for n in range(N_W13, N_W13 + 3):
                load_chunk(n)
            store_xs(B, 0)
            for n in range(N_W13 + 3, NW):
                load_chunk(n)
            sp.wait_ge(sem("pad_ready"), 1)
            _, ends = nc.values_load_multi_w_load_instructions(
                pad_i[0:1, :], engines=[mybir.EngineType.SP], min_val=0, max_val=NE * ROWS - P,
                skip_runtime_bounds_check_because=MADE_ON_CHIP)
            for n in range(NE):
                sp.dma_start(row_tab[ds(ends[n], P), :], pad_tab[n * P:(n + 1) * P, :]
                             ).then_inc(sem("pads_stored"), 16)
            sp.wait_ge(sem("pads_stored"), 16 * (NE + 2))
            sp.wait_ge(sem("table_done"), 1)
            for par in (0, 1):
                sp.wait_ge(sem(f"rows_stored{par}"), 64 * (NP // 2))

            def load_rows(n, u):
                r = sp.value_load(tab_r[0:1, ds(n, 1)], min_val=0, max_val=NE * ROWS + (SPARE - NE - 1) * P)
                wait(sp, f"scattered{u}", (n - u) * 16 // RING if isinstance(n, int) else (n - u) * 2)
                sp.dma_start(rows[:, u, :], row_tab[ds(r, P), :]).then_inc(sem(f"rows_loaded{u}"), 16)

            sp.wait_ge(sem("vlo_done"), NP + 1)
            for u in range(RING):
                load_rows(u, u)
            store_xs(B, 1)
            for par in (0, 1):
                sp.wait_ge(sem(f"xs_stored{par}"), 16 * (NP // 2))
            with sp.Fori(1, NBLK // RING) as i:
                for u in range(RING):
                    load_rows(i * RING + u, u)
                for t in (-2, -1):
                    pair = sp.snap(i * 2 + t)
                    row = first_row(pair)
                    sp.dma_start(acc[:, ds(pair, 1), :, :].rearrange("p a t d -> p (a t) d"),
                                 xs_tab[ds(row, 2 * P), :].rearrange("(t p) d -> p t d", p=P)
                                 ).then_inc(sem("acc_loaded"), 16)
            for u in range(RING):
                sp.wait_ge(sem(f"scattered{u}"), 16 * (NBLK // RING))

            def load_parts(pair, u):
                rows_ = [first_row(pair), first_row(pair + T // (2 * P))]
                wait(sp, "combined", pair - PARTS + 1)
                for k in range(2):
                    sp.dma_start(cx[:, u, k, :, :],
                                 exp_tab[ds(rows_[k], 2 * P), :].rearrange("(t p) d -> p t d", p=P)
                                 ).then_inc(sem(f"parts_loaded{u}"), 16)

            for u in range(PARTS):
                load_parts(u, u)
            with sp.Fori(1, NP // PARTS) as i:
                for u in range(PARTS):
                    load_parts(i * PARTS + u, u)
            sp.wait_ge(sem("out_stored"), 16 * NP)

        @block.tensor
        def _(pe):
            Y16 = g_banks[0].bitcast(f16)

            def qk(b, j, a):
                s = b * SLOTS + j
                wait(pe, "qlo_done", s + 1)
                wait(pe, "xlo_done", s + 1)
                wait(pe, "pexp_done", 2 * s + a)
                n = (j + 1) * 2 * P
                for c in range(0, n, 512):
                    w = min(512, n - c)
                    dst = s_banks[c // 512][:, 0:w]
                    for k in range(KD):
                        ins = products(pe, dst,
                                       lambda hl: qT[:, hl, j % 2, k, a * P:(a + 1) * P],
                                       lambda hl: xT[:, hl, k, c:c + w],
                                       first=k == 0, last=k == KD - 1 and c + w < n)
                    if c + w == n:
                        ins = pe.matmul(s_banks[c // 512][:, w - 2 * P:w], identr[:, :], mask[:, a, :],
                                        start=False, stop=True)
                ins.then_inc(sem("qk_done"), 1)

            def down(b, j, t):
                p = b * SLOTS + j - 2
                wait(pe, "hlo_done", (UNITS - 1) * (p + 1))
                wait(pe, "hlast_done", p + 1)
                wait(pe, "pTlo_done", chunks_before(b, j, 0) if not isinstance(b, int) or b < B
                     else chunks_before(B, 0, 0))
                if j >= 2 and t == 0:
                    wait(pe, "prefix_read", p + 1)
                if j < 2:
                    wait(pe, "xs_done", 2 * p)
                for k in range(UNITS):
                    q0 = 64 if k == UNITS - 1 else 0
                    ins = products(pe, down_out(j, t),
                                   lambda hl: hT[q0:P, hl, k, t * P:(t + 1) * P],
                                   lambda hl: wS[q0:P, hl, k, :],
                                   first=k == 0, last=k == UNITS - 1)
                ins.then_inc(sem("down_done"), 1)

            def transpose_y(b, j):
                p = b * SLOTS + j - 1
                wait(pe, "h_done", UNITS * p - 1)
                wait(pe, "y16lo_done", p + 1)
                for hl in range(2):
                    for k in range(KD):
                        for t in range(2):
                            o = hl * 512 + k * 256 + t * P
                            src = y16[:, (j + 1) % 2, 0, t, hl * D + k * P:hl * D + (k + 1) * P]
                            ins = pe.transpose(Y16[:, o:o + P], src, ident16[:, :])
                ins.then_inc(sem("yT_tp"), 1)

            def transpose_x(b, j):
                q = b * SLOTS + j + 1
                wait(pe, "vlo_done", q)
                wait(pe, "xn_done", q + 1)
                for k in range(KD):
                    for t in range(2):
                        o = k * 256 + t * P
                        ins = pe.transpose(x_bank[:, o:o + P], nx[:, t, k * P:(k + 1) * P], identf[:, :])
                ins.then_inc(sem("xT_tp"), 1)

            def transpose_p(b, j, a):
                g = (b * SLOTS + j) * 2 + a
                wait(pe, "pexp_done", g + 1)
                if a == 0:
                    if j >= 2:
                        wait(pe, "xs_done", g - 2)
                    wait(pe, "prefix_read", b * SLOTS + j - 1)
                wait(pe, "pTlo_done", chunks_before(b, j, a))
                for c0, c1 in chunks_of(j, a):
                    for kb in range(c0, c1):
                        ins = pe.transpose(probsT[:, kb * P:(kb + 1) * P],
                                           p32[:, kb * P:(kb + 1) * P], identf[:, :])
                    ins.then_inc(sem("pT_tp"), 1)

            def logits(b, j, last):
                s = b * SLOTS + j
                wait(pe, "yT_done", s)
                if last:
                    wait(pe, "vlo_done", s + 1)
                else:
                    wait(pe, "xg_done", s + 2)
                for t in range(2):
                    for k in range(KD):
                        pe.matmul(x_bank[:, t * 20:(t + 1) * 20], yT[:, 0, k, t * P:(t + 1) * P],
                                  wR[:, k, :, :].rearrange("p h n -> p (h n)"), start=k == 0, stop=False)
                        ins = pe.matmul(x_bank[:, t * 20:t * 20 + 10], yT[:, 1, k, t * P:(t + 1) * P],
                                        wR[:, k, 0, :], start=False, stop=k == KD - 1)
                ins.then_inc(sem("logits_done"), 1)

            def prefix(b, j):
                p = b * SLOTS + j - 2
                wait(pe, "mask_done", p + 1)
                wait(pe, "pTlo_done", chunks_before(*((B, 0) if b == B else (b, j)), 0) if isinstance(b, int)
                     else chunks_before(b, j, 0))
                dst = t_banks[0][:, 0:2 * NE]
                pe.matmul(dst, upper[:, :], mk[:, :, :].rearrange("p t e -> p (t e)"), start=True, stop=False)
                pe.matmul(dst, ones[:, :], cum[:, j % 2, 0:2, :].rearrange("p t e -> p (t e)"),
                          start=False, stop=True).then_inc(sem("prefix_done"), 1)

            def pv(b, j, a):
                g = (b * SLOTS + j) * 2 + a
                wait(pe, "pTlo_done", chunks_before(b, j, a) + len(chunks_of(j, a)))
                wait(pe, "vlo_done", b * SLOTS + j + 1)
                wait(pe, "x1_done", g)
                n = 2 * j + a + 1
                for kb in range(n):
                    ins = products(pe, o_bank[:, a * D:(a + 1) * D],
                                   lambda hl: pT[:, hl, kb, :], lambda hl: vp[:, hl, kb, :],
                                   first=kb == 0, last=kb == n - 1)
                ins.then_inc(sem("pv_done"), 1)

            def unit(b, j, u):
                p = b * SLOTS + j - 1
                wait(pe, "yT_done", p + 1)
                wait(pe, "h_done", UNITS * p + u - 1)
                g = g_banks[u % 2]
                for i in range(1 if u == UNITS - 1 else 2):
                    for k in range(KD):
                        c = u * 2 * P + i * P
                        ins = products(pe, g[:, i * 256:(i + 1) * 256],
                                       lambda hl: wG[:, hl, k, c:c + P], lambda hl: yT[:, hl, k, :],
                                       first=k == 0, last=k == KD - 1)
                ins.then_inc(sem("gu_done"), 1)

            def q_proj(b, j):
                q = b * SLOTS + j + 1
                wait(pe, "xlo_done", q + 1)
                wait(pe, "logits_read", q - 1)
                c = ((j + 1) % SLOTS) * 2 * P
                for m in range(KD):
                    for k in range(KD):
                        ins = products(pe, x_bank[:, m * 256:(m + 1) * 256],
                                       lambda hl: wA[:, hl, k, m * P:(m + 1) * P],
                                       lambda hl: xT[:, hl, k, c:c + 2 * P], first=k == 0, last=k == KD - 1)
                ins.then_inc(sem("q_done"), 1)

            def v_proj(b, j):
                q = b * SLOTS + j + 1
                wait(pe, "qlo_done", q + 1)
                c = ((j + 1) % SLOTS) * 2 * P
                for t in range(2):
                    for k in range(KD):
                        ins = products(pe, x_bank[:, t * 256:(t + 1) * 256],
                                       lambda hl: xT[:, hl, k, c + t * P:c + (t + 1) * P],
                                       lambda hl: wV[:, hl, k, :], first=k == 0, last=k == KD - 1)
                ins.then_inc(sem("v_done"), 1)

            pe.wait_ge(sem("qkv_loaded"), 64)
            for n, (l, r) in enumerate(((0, 1), (2, 3))):
                for m in range(KD):
                    for k in range(KD):
                        ins = pe.matmul(banks[n][:, m * 256:(m + 1) * 256], w_raw[l][:, k, m * P:(m + 1) * P],
                                        w_raw[r][:, k, :], start=k == 0, stop=k == KD - 1)
                ins.then_inc(sem("wprod_done"), 1)
            pe.wait_ge(sem("consts_done"), 1)
            transpose_x(0, -1)
            pe.wait_ge(sem("wprod_split"), 2)
            q_proj(0, -1)
            v_proj(0, -1)

            def slot(b, j, last=False):
                s = b * SLOTS + j
                behind, behind2 = (not isinstance(s, int) or s >= n for n in (1, 2))
                if not last:
                    qk(b, j, 0)
                if behind2:
                    prefix(b, j)
                    down(b, j, 0)
                if not last and j < 2:
                    transpose_p(b, j, 0)
                if behind2:
                    down(b, j, 1)
                if behind:
                    transpose_y(b, j)
                if not last:
                    transpose_x(b, j)
                    if j >= 2:
                        transpose_p(b, j, 0)
                    qk(b, j, 1)
                    pv(b, j, 0)
                if behind:
                    logits(b, j, last)
                    if isinstance(s, int) and s == 1:
                        pe.wait_ge(sem("w_split"), N_FFN)
                    unit(b, j, 0)
                    unit(b, j, 1)
                if not last:
                    transpose_p(b, j, 1)
                if behind:
                    unit(b, j, 2)
                if last:
                    prefix(B, 1)
                    pe.wait_ge(sem("pexp_done"), 2 * NP)
                    pe.matmul(s_banks[0][:, 0:NE], ones[:, :], cum[:, (NP - 1) % 2, 2, :], start=True, stop=True
                              ).then_inc(sem("count_done"), 1)
                if behind:
                    unit(b, j, 3)
                if not last:
                    q_proj(b, j)
                if behind:
                    unit(b, j, 4)
                    unit(b, j, 5)
                if not last:
                    pv(b, j, 1)
                    v_proj(b, j)

            slots(pe, slot)
            slot(B, 0, last=True)
            down(B, 1, 0)
            down(B, 1, 1)

            def rows_T(n, u, m):
                wait(pe, f"rows_loaded{u}", (m + 1) * 16)
                wait(pe, "rT_done", n - 1)
                for hl in range(2):
                    for k in range(KD):
                        o = hl * 256 + k * P
                        ins = pe.transpose(banks[u % 2].bitcast(f16)[:, o:o + P],
                                           rows[:, u, hl * D + k * P:hl * D + (k + 1) * P], ident16[:, :])
                ins.then_inc(sem("rT_tp"), 1)

            def expert_gu(n, u, e_):
                wait(pe, "rT_done", n + 1)
                wait(pe, "eh_done", n - 1)
                for k in range(KD):
                    ins = products(pe, banks[2 + u % 2][:, 0:2 * FE], lambda hl: rT[:, u % 2, hl, k, :],
                                   lambda hl: wE[:, hl, ds(e_, 1), k, :].rearrange("p a n -> p (a n)"),
                                   first=k == 0, last=k == KD - 1)
                ins.then_inc(sem("egu_done"), 1)

            def inner_T(n, u):
                wait(pe, "eh_done", n + 1)
                wait(pe, "ehT_done", n - 1)
                for c in range(2):
                    ins = pe.transpose(banks[4 + u % 2][0:FH, c * P:(c + 1) * P],
                                       eh[:, u % 2, c * FH:(c + 1) * FH], identf[:, :])
                ins.then_inc(sem("ehT_tp"), 1)

            def expert_down(n, u, e_):
                wait(pe, "ehT_done", n + 1)
                wait(pe, "eo_done", n - 1)
                for c in range(2):
                    ins = products(pe, banks[6 + u % 2][:, 0:D], lambda hl: ehT[0:FH, u % 2, hl, c, :],
                                   lambda hl: w2s[0:FH, hl, ds(e_, 1), c, :].rearrange("p a n -> p (a n)"),
                                   first=c == 0, last=c == 1)
                ins.then_inc(sem("edown_done"), 1)

            def experts_of(first, count):
                _, values = nc.values_load_multi_w_load_instructions(
                    tab_e[0:1, ds(first, count)], engines=[mybir.EngineType.PE], min_val=0, max_val=NE - 1,
                    skip_runtime_bounds_check_because=MADE_ON_CHIP)
                return values

            def steps(first, m, count, experts):
                for u in range(count):
                    n = first + u
                    known = isinstance(n, int)
                    if not known or n < NBLK:
                        expert_gu(n, u % RING, experts[u + 2])
                    if not known or n + 2 < NBLK:
                        rows_T(n + 2, (u + 2) % RING, m + (u + 2) // RING)
                    if not known or 0 <= n - 1 < NBLK:
                        inner_T(n - 1, (u - 1) % RING)
                    if known and n == 2:
                        pe.wait_ge(sem("w_split"), NW)
                    if not known or 0 <= n - 2 < NBLK:
                        expert_down(n - 2, (u - 2) % RING, experts[u])

            pe.wait_ge(sem("xs_done"), 2 * NP)
            pe.wait_ge(sem("table_done"), 1)
            rows_T(0, 0, 0)
            rows_T(1, 1, 0)
            steps(0, 0, RING, [None, None, *experts_of(0, RING)])
            with pe.Fori(1, NBLK // RING - 1) as i:
                steps(i * RING, i, RING, experts_of(i * RING - 2, RING + 2))
            steps(NBLK - RING, NBLK // RING - 1, RING + 2, experts_of(NBLK - RING - 2, RING + 2))

        @block.scalar
        def _(act):
            Y16 = g_banks[0].bitcast(f16)

            def exps(b, j, a):
                g = (b * SLOTS + j) * 2 + a
                n = 2 * j + a + 1
                wait(act, "nmax_done", g + 1)
                wait(act, "pT_tp", chunks_before(b, j, a))
                act.activation(p32[:, 0:n * P], scores[:, 0:n * P], ACT.Exp, bias=nmax[:, a:a + 1], scale=SCALE,
                               accum_out=rsum[:, a:a + 1]).then_inc(sem("pexp_done"), 1)

            def y_hi(b, j):
                p = b * SLOTS + j - 1
                par = (j + 1) % 2
                wait(act, "yn_done", p + 1)
                if not isinstance(p, int):
                    act.wait_ge(sem(f"rows_stored{par}"), (p - 2 - par) * 32 + 64)
                elif p >= 2:
                    act.wait_ge(sem(f"rows_stored{par}"), ((p - 2) // 2 + 1) * 64)
                if isinstance(p, int) and p < 2:
                    act.wait_ge(sem("pads_stored"), 32)
                act.activation(y16[:, par, 0, :, 0:D], ny[:, :, :], ACT.Copy).then_inc(sem("y16hi_done"), 1)

            def y_T(b, j):
                p = b * SLOTS + j - 1
                wait(act, "yT_tp", p + 1)
                wait(act, "gu_done", UNITS * p)
                act.activation(yT[:, :, :, :].rearrange("p h k n -> p (h k n)"), Y16[:, :], ACT.Copy,
                               scale=1.0 / UP).then_inc(sem("yT_done"), 1)

            def p_T(b, j, a):
                g = (b * SLOTS + j) * 2 + a
                wait(act, "pv_done", g)
                for i, (c0, c1) in enumerate(chunks_of(j, a)):
                    wait(act, "pT_tp", chunks_before(b, j, a) + i + 1)
                    act.activation(pT[:, 0, c0:c1, :].rearrange("p k q -> p (k q)"),
                                   probsT[:, c0 * P:c1 * P], ACT.Copy).then_inc(sem("pThi_done"), 1)

            def route_acts(b, j):
                p = b * SLOTS + j - 1
                wait(act, "shifted_done", p + 1)
                act.activation(tg[:, :], lg[:, :, 8], ACT.Tanh, scale=0.5)
                act.activation(ex[:, :, :], sh[:, :, :], ACT.Exp).then_inc(sem("rexp_done"), 1)

            def x_gamma(b, j):
                q = b * SLOTS + j + 1
                wait(act, "xT_tp", q + 1)
                wait(act, "xlo_done", q)
                for k in range(KD):
                    ins = act.activation(xg[:, k, :], x_bank[:, k * 256:(k + 1) * 256], ACT.Identity,
                                         scale=gam[:, 0, k:k + 1], bias=gam[:, 1, k:k + 1])
                ins.then_inc(sem("xg_done"), 1)

            def x_hi(b, j):
                q = b * SLOTS + j + 1
                c = ((j + 1) % SLOTS) * 2 * P
                wait(act, "xg_done", q + 1)
                if j == SLOTS - 1:
                    wait(act, "qk_done", 2 * q)
                act.activation(xT[:, 0, :, c:c + 2 * P], xg[:, :, :], ACT.Copy).then_inc(sem("xhi_done"), 1)

            def q_hi(b, j):
                q = b * SLOTS + j + 1
                wait(act, "q_done", q + 1)
                act.activation(qT[:, 0, (j + 1) % 2, :, :].rearrange("p k n -> p (k n)"), x_bank[:, :], ACT.Copy
                               ).then_inc(sem("qhi_done"), 1)

            def v_hi(b, j):
                q = b * SLOTS + j + 1
                c = ((j + 1) % SLOTS) * 2
                wait(act, "v_done", q + 1)
                act.activation(vp[:, 0, c:c + 2, :].rearrange("p k n -> p (k n)"), x_bank[:, :], ACT.Copy
                               ).then_inc(sem("vhi_done"), 1)

            def unit_tanh(b, j, u):
                p = b * SLOTS + j - 1
                wait(act, "gu_done", UNITS * p + u + 1)
                wait(act, "h_done", UNITS * p + u - 1)
                m = 64 if u == UNITS - 1 else P
                act.activation(th[0:m, u % 2, :], g_banks[u % 2][0:m, 0:256], ACT.Tanh, scale=0.5
                               ).then_inc(sem("th_done"), 1)

            def h_hi(b, j, u):
                p = b * SLOTS + j - 1
                wait(act, "h_done", UNITS * p + u + 1)
                wait(act, "down_done", 2 * p)
                q0 = 64 if u == UNITS - 1 else 0
                act.activation(hT[q0:P, 0, u, :], h32[q0:P, u % 2, :], ACT.Copy).then_inc(sem("hhi_done"), 1)

            def w2_turn(first, end):
                for n in range(first, end):
                    split(N_W13 + n)

            def slot(b, j, last=False):
                s = b * SLOTS + j
                behind = not isinstance(s, int) or s >= 1
                if behind:
                    y_hi(b, j)
                if not last:
                    exps(b, j, 0)
                if j < 2 and not last:
                    p_T(b, j, 0)
                if behind:
                    y_T(b, j)
                if last:
                    act.wait_ge(sem("vlo_done"), NP + 1)
                    w2_turn(0, 3)
                if not last:
                    if j >= 2:
                        p_T(b, j, 0)
                    x_gamma(b, j)
                    x_hi(b, j)
                    exps(b, j, 1)
                if behind:
                    route_acts(b, j)
                    unit_tanh(b, j, 0)
                    unit_tanh(b, j, 1)
                    h_hi(b, j, 0)
                if not last:
                    p_T(b, j, 1)
                if behind:
                    h_hi(b, j, 1)
                if last:
                    w2_turn(3, 5)
                if behind:
                    unit_tanh(b, j, 2)
                    h_hi(b, j, 2)
                    unit_tanh(b, j, 3)
                if not last:
                    q_hi(b, j)
                if behind:
                    h_hi(b, j, 3)
                    unit_tanh(b, j, 4)
                    unit_tanh(b, j, 5)
                    h_hi(b, j, 4)
                    h_hi(b, j, 5)
                if last:
                    w2_turn(5, NE)
                if not last:
                    v_hi(b, j)
                if s in turns if isinstance(s, int) else False:
                    for n in turns[s]:
                        split(n)

            def split(n):
                act.wait_ge(sem(f"w_loaded{n % 3}"), 16 * (n // 3 + 1))
                act.activation(halves(n, 0), staged(n), ACT.Copy).then_inc(sem("w_hi"), 1)

            for n in range(2):
                act.wait_ge(sem("wprod_done"), n + 1)
                act.activation((wA, wV)[n][:, 0, :, :].rearrange("p k n -> p (k n)"), banks[n][:, :], ACT.Copy
                               ).then_inc(sem("wprod_hi"), 1)
            act.wait_ge(sem("gam_done"), 1)
            x_gamma(0, -1)
            x_hi(0, -1)
            q_hi(0, -1)
            v_hi(0, -1)
            slots(act, slot)
            slot(B, 0, last=True)

            def rT_copy(n, v):
                wait(act, "rT_tp", n + 1)
                wait(act, "egu_done", n - 1)
                act.activation(rT[:, v, :, :, :].rearrange("p h k n -> p (h k n)"),
                               banks[v].bitcast(f16)[:, 0:512], ACT.Copy, scale=1.0 / UP
                               ).then_inc(sem("rT_done"), 1)

            def step(n, u):
                known = isinstance(n, int)
                if not known or n < NBLK:
                    wait(act, "egu_done", n + 1)
                    wait(act, "eh_done", n - 1)
                    act.activation(eth[:, u % 2, :], banks[2 + u % 2][:, 0:FE], ACT.Tanh, scale=0.5
                                   ).then_inc(sem("eth_done"), 1)
                if not known or n + 2 < NBLK:
                    rT_copy(n + 2, u % 2)
                if not known or 0 <= n - 1 < NBLK:
                    v = (u - 1) % 2
                    wait(act, "ehT_tp", n)
                    wait(act, "edown_done", n - 2)
                    act.activation(ehT[0:FH, v, 0, :, :].rearrange("p k n -> p (k n)"), banks[4 + v][0:FH, 0:256],
                                   ACT.Copy).then_inc(sem("ehThi_done"), 1)

            rT_copy(0, 0)
            rT_copy(1, 1)
            for n in range(RING):
                step(n, n)
            with act.Fori(1, NBLK // RING - 1) as i:
                for u in range(RING):
                    step(i * RING + u, u)
            for n in range(NBLK - RING, NBLK + 1):
                step(n, n % RING)

            def store_out(pair):
                row = act.snap(pair * 2 * P)
                act.wait_ge(sem("combined"), pair + 1)
                act.dma_start(out[ds(row, 2 * P), :].rearrange("(t p) d -> p t d", p=P),
                              acc[:, ds(pair, 1), :, :].rearrange("p a t d -> p (a t) d")
                              ).then_inc(sem("out_stored"), 16)

            with act.Fori(0, NP // PARTS) as i:
                for u in range(PARTS):
                    store_out(i * PARTS + u)

        @block.vector
        def _(dve):
            ts, tt, stt = dve.tensor_scalar, dve.tensor_tensor, dve.scalar_tensor_tensor

            def x_stats(b, j, k=2):
                q = b * SLOTS + j + k
                par = (j + k) % 2
                loads = (b * SLOTS + (j + k) - par) * 8 + 16
                wait(dve, f"x_loaded{par}", loads)
                link, n = chained(dve, "xstat_steps", 2, q)
                dve.bn_stats(st[:, 0, :], x_in[:, par, 0, :])
                link(dve.bn_stats(st[:, 1, :], x_in[:, par, 1, :]))
                wait(dve, "xn_done", q - 1)
                dve.memset(idle_dve[:, :], 0.0)
                dve.bn_aggr(mv1[:, par, 0, :], st[:, 0, :])
                link(dve.bn_aggr(mv1[:, par, 1, :], st[:, 1, :]))
                assert n[0] == 2
                wait(dve, "xpow_done", q)
                ts(b1[:, 0, :], mv1[:, par, :, 1], EPS, None, ALU.add)
                ts(b1[:, 1, :], mv1[:, par, :, 1], 1 + EPS, EPS * EPS, ALU.mult, ALU.add
                   ).then_inc(sem("xbase_done"), 1)

            def x_norm(b, j):
                q = b * SLOTS + j + 1
                par = (j + 1) % 2
                wait(dve, "xpow_done", q + 1)
                wait(dve, "x1_done", 2 * (q - 1))
                wait(dve, "xT_tp", q)
                for t in range(2):
                    ins = ts(nx[:, t, :], x_in[:, par, t, :], mv1[:, par, t, 0:1], r1[:, par, 1, t:t + 1],
                             ALU.subtract, ALU.mult)
                ins.then_inc(sem("xn_done"), 1)
                wait(dve, "xn_done", q + 1)
                for t in range(2):
                    ins = stt(xz[:, par, t, :], nx[:, t, :], ratio[:, par, t:t + 1], x_in[:, par, t, :],
                              ALU.mult, ALU.add)
                ins.then_inc(sem("xz_done"), 1)

            def q_lo(b, j):
                q = b * SLOTS + j + 1
                wait(dve, "qhi_done", q + 1)
                flat = lambda hl: qT[:, hl, (j + 1) % 2, :, :].rearrange("p k n -> p (k n)")
                tt(flat(1), x_bank[:, :], flat(0).bitcast(f32), ALU.subtract).then_inc(sem("qlo_done"), 1)

            def v_lo(b, j):
                q = b * SLOTS + j + 1
                c = ((j + 1) % SLOTS) * 2
                wait(dve, "vhi_done", q + 1)
                flat = lambda hl: vp[:, hl, c:c + 2, :].rearrange("p k n -> p (k n)")
                tt(flat(1), x_bank[:, :], flat(0).bitcast(f32), ALU.subtract).then_inc(sem("vlo_done"), 1)

            def row_max(b, j, a):
                g = (b * SLOTS + j) * 2 + a
                n = (2 * j + a + 1) * P
                wait(dve, "qk_done", g + 1)
                dve.tensor_reduce(rmax[:, a:a + 1], scores[:, 0:n], AX.X, ALU.max).then_inc(sem("rmax_done"), 1)
                wait(dve, "rmax_done", g + 1)
                ts(nmax[:, a:a + 1], rmax[:, a:a + 1], -SCALE, None, ALU.mult
                   ).then_inc(sem("nmax_done"), 1)

            def pT_lo(b, j, a, i):
                c0, c1 = chunks_of(j, a)[i]
                wait(dve, "pThi_done", chunks_before(b, j, a) + i + 1)
                flat = lambda hl: pT[:, hl, c0:c1, :].rearrange("p k q -> p (k q)")
                tt(flat(1), probsT[:, c0 * P:c1 * P], flat(0).bitcast(f32), ALU.subtract
                   ).then_inc(sem("pTlo_done"), 1)

            def attended(b, j, a, between=lambda i: None):
                s = b * SLOTS + j
                g = s * 2 + a
                par, ring = j % 2, j % 4
                dve.reciprocal(rinv[:, a:a + 1], rsum[:, a:a + 1]).then_inc(sem("rinv_done"), 1)
                between(0)
                wait(dve, "rinv_done", g + 1)
                wait(dve, "pv_done", g + 1)
                wait(dve, "xz_done", s + 1)
                if not isinstance(s, int):
                    dve.wait_ge(sem(f"xs_stored{par}"), (s - 4 - par) * 8 + 16)
                elif s >= 4:
                    dve.wait_ge(sem(f"xs_stored{par}"), ((s - 4) // 2 + 1) * 16)
                stt(x1[:, ring, a, :], o_bank[:, a * D:(a + 1) * D], rinv[:, a:a + 1], xz[:, par, a, :],
                    ALU.mult, ALU.add).then_inc(sem("x1_done"), 1)
                between(1)
                wait(dve, "x1_done", g + 1)
                dve.bn_stats(st[:, 2 + a, :], x1[:, ring, a, :]).then_inc(sem("st2_done"), 1)
                between(2)
                wait(dve, "st2_done", g + 1)
                dve.memset(idle_dve[:, :], 0.0)
                dve.bn_aggr(mv2[:, par, a, :], st[:, 2 + a, :]).then_inc(sem("mv2_done"), 1)
                if a == 1:
                    between(3)
                    wait(dve, "mv2_done", g + 1)
                    wait(dve, "ypow_done", s)
                    ts(b2[:, :], mv2[:, par, :, 1], EPS, 1.0 / UP / UP, ALU.add, ALU.mult
                       ).then_inc(sem("ybase_done"), 1)

            def y_norm(b, j):
                p = b * SLOTS + j - 1
                par, ring = (j + 1) % 2, (j + 3) % 4
                wait(dve, "ypow_done", p + 1)
                wait(dve, "y16lo_done", p)
                for t in range(2):
                    ins = ts(ny[:, t, :], x1[:, ring, t, :], mv2[:, par, t, 0:1], r2[:, par, t:t + 1],
                             ALU.subtract, ALU.mult)
                ins.then_inc(sem("yn_done"), 1)

            def y_rows(b, j):
                p = b * SLOTS + j - 1
                par = (j + 1) % 2
                wait(dve, "y16lo_done", p + 1)
                dve.tensor_copy(y16[:, par, 1, :, 0:2 * D], y16[:, par, 0, :, 0:2 * D])
                ids = y16[:, par, :, :, :].bitcast(i32)[:, :, :, D]
                dve.tensor_copy(ids, idtab[:, ds(p, 1), :, :].rearrange("p a k t -> p (a k) t")
                                ).then_inc(sem("rows_ready"), 1)

            def shared_sum(b, j, t):
                p = b * SLOTS + j - 2
                wait(dve, "down_done", 2 * p + (2 if j < 2 else t + 1))
                row = x1[:, (j + 2) % 4, t, :]
                stt(row, down_out(j, t), sg[:, j % 2, t:t + 1], row, ALU.mult, ALU.add
                    ).then_inc(sem("xs_done"), 1)

            ROUTE = 16

            def route_a(b, j):
                p = b * SLOTS + j - 1
                wait(dve, "logits_done", p + 1)
                wait(dve, "mask_done", p)
                parts = x_bank[:, 0:40].rearrange("p (t h n) -> p t h n", t=2, h=2)
                dve.tensor_copy(lg[:, :, :], parts[:, :, 1, :]).then_inc(sem("logits_half"), 1)
                wait(dve, "logits_half", p + 1)
                tt(lg[:, :, :], parts[:, :, 0, :], lg[:, :, :], ALU.add).then_inc(sem("logits_read"), 1)
                wait(dve, "logits_read", p + 1)
                link, c = chained(dve, "ra_steps", 1, p)
                link(dve.tensor_reduce(small[:, 0, :], lg[:, :, 0:NE], AX.X, ALU.max))
                tt(sh[:, :, :], lg[:, :, 0:NE], bc(small[:, 0, :], NE), ALU.subtract
                   ).then_inc(sem("shifted_done"), 1)

            def route_b(b, j, *steps):
                p = b * SLOTS + j - 1
                par = (j + 1) % 2
                for i in steps:
                    if i == 0:
                        wait(dve, "rexp_done", p + 1)
                        wait(dve, "prefix_done", p)
                    else:
                        wait(dve, "rb_steps", p * ROUTE + i)
                    k, m = divmod(i - 3, 6)
                    if i == 0:
                        ins = dve.tensor_reduce(small[:, 1, :], ex[:, :, :], AX.X, ALU.add)
                    elif i == 1:
                        ins = dve.reciprocal(small[:, 2, :], small[:, 1, :])
                    elif i == 2:
                        ins = tt(pr[:, :, :], ex[:, :, :], bc(small[:, 2, :], NE), ALU.mult)
                    elif i == 14:
                        dve.tensor_copy(wts[:, ds(p, 1), :, :].rearrange("p a k t -> p (a k) t"), vtmp[:, :, :])
                        ts(sg[:, par, :], tg[:, :], 1.0, 0.5, ALU.add, ALU.mult)
                        tt(mk[:, :, :], one[:, 0, :, :], one[:, 1, :, :], ALU.add)
                        ins = dve.tensor_copy(cum[:, par, 0, :], cum[:, 1 - par, 2, :])
                    elif i == 15:
                        ins = tt(cum[:, par, 1, :], cum[:, par, 0, :], mk[:, 0, :], ALU.add)
                    elif i == 16:
                        tt(cum[:, par, 2, :], cum[:, par, 1, :], mk[:, 1, :], ALU.add).then_inc(sem("mask_done"), 1)
                        continue
                    elif m == 0:
                        ins = dve.tensor_reduce(vtmp[:, k, :], pr[:, :, :], AX.X, ALU.max)
                    elif m == 1:
                        ins = tt(ca[:, :, :], pr[:, :, :], bc(vtmp[:, k, :], NE), ALU.is_equal)
                    elif m == 2:
                        ins = tt(cb[:, :, :], ca[:, :, :], w8[:, :, :], ALU.mult)
                    elif m == 3:
                        ins = dve.tensor_reduce(small[:, 3, :], cb[:, :, :], AX.X, ALU.max)
                    elif m == 4:
                        ins = tt(one[:, k, :, :], cb[:, :, :], bc(small[:, 3, :], NE), ALU.is_equal)
                    else:
                        ins = stt(pr[:, :, :], one[:, 0, :, :], -2.0, pr[:, :, :], ALU.mult, ALU.add)
                    ins.then_inc(sem("rb_steps"), 1)

            def route_c(b, j):
                p = b * SLOTS + j - 2
                par = j % 2
                wait(dve, "prefix_done", p + 1)
                tt(dd[:, :, :], t_banks[0][:, 0:2 * NE].rearrange("p (t e) -> p t e", t=2), eoff[:, :, :], ALU.add
                   ).then_inc(sem("prefix_read"), 1)
                wait(dve, "prefix_read", p + 1)
                link, c = chained(dve, "rc_steps", 2, p)
                tt(ca[:, :, :], dd[:, :, :], one[:, 0, :, :], ALU.mult)
                link(tt(cb[:, :, :], dd[:, :, :], one[:, 1, :, :], ALU.mult))
                dve.tensor_reduce(df[:, 0, :], ca[:, :, :], AX.X, ALU.add)
                link(dve.tensor_reduce(df[:, 1, :], cb[:, :, :], AX.X, ALU.add))
                dve.tensor_copy(di[:, par, :, :], df[:, :, :]).then_inc(sem("dest_done"), 1)
                assert c[0] == 2

            def unit_a(b, j, u):
                p = b * SLOTS + j - 1
                m = 64 if u == UNITS - 1 else P
                wait(dve, "th_done", UNITS * p + u + 1)
                a = th[64:P, 1, :] if u == UNITS - 1 else th[:, u % 2, :]
                stt(a, th[0:m, u % 2, :], 1.0, g_banks[u % 2][0:m, 0:256], ALU.add, ALU.mult
                    ).then_inc(sem("ha_done"), 1)

            def unit_b(b, j, u):
                p = b * SLOTS + j - 1
                g = g_banks[u % 2]
                m = 64 if u == UNITS - 1 else P
                wait(dve, "hlo_done", (UNITS - 1) * p + max(u - 1, 0))
                wait(dve, "hhi_done", UNITS * p + u - 1)
                wait(dve, "ha_done", UNITS * p + u + 1)
                up = g[64:P, 0:256] if u == UNITS - 1 else g[:, 256:512]
                a = th[64:P, 1, :] if u == UNITS - 1 else th[:, u % 2, :]
                stt(h32[P - m:P, u % 2, :], a, 0.5, up, ALU.mult, ALU.mult).then_inc(sem("h_done"), 1)

            def last_lo(b, j):
                p = b * SLOTS + j - 1
                wait(dve, "hhi_done", UNITS * (p + 1))
                u = UNITS - 1
                tt(hT[64:P, 1, u, :], h32[64:P, u % 2, :], hT[64:P, 0, u, :].bitcast(f32), ALU.subtract
                   ).then_inc(sem("hlast_done"), 1)

            def split(n):
                dve.wait_ge(sem("w_hi"), n + 1)
                tt(halves(n, 1), staged(n), halves(n, 0).bitcast(f32), ALU.subtract).then_inc(sem("w_split"), 1)

            def w2_turn(first, end):
                for n in range(first, end):
                    split(N_W13 + n)

            def slot(b, j):
                s = b * SLOTS + j
                behind, behind2 = (not isinstance(s, int) or s >= n for n in (1, 2))
                if j == 0:
                    row_max(b, j, 0)
                if behind2 and j >= 2:
                    route_c(b, j)
                if behind:
                    y_norm(b, j)
                if j > 0:
                    row_max(b, j, 0)
                if behind2 and j < 2:
                    route_c(b, j)
                v_lo(b, j - 1)
                if behind2 and j >= 2:
                    shared_sum(b, j, 0)
                if j < 2:
                    pT_lo(b, j, 0, 0)
                x_norm(b, j)
                if behind2:
                    if j < 2:
                        shared_sum(b, j, 0)
                    shared_sum(b, j, 1)
                if behind:
                    y_rows(b, j)
                if j >= 2:
                    for i in range(len(chunks_of(j, 0))):
                        pT_lo(b, j, 0, i)
                row_max(b, j, 1)
                if behind:
                    route_a(b, j)
                attended(b, j, 0)
                if behind:
                    for u in range(2):
                        unit_a(b, j, u)
                        route_b(b, j, 2 * u)
                        unit_b(b, j, u)
                        route_b(b, j, 2 * u + 1)
                for i in range(len(chunks_of(j, 1))):
                    pT_lo(b, j, 1, i)
                    if behind:
                        route_b(b, j, 4 + i)
                if behind:
                    route_b(b, j, *range(4 + len(chunks_of(j, 1)), 6))
                    unit_a(b, j, 2)
                    route_b(b, j, 6)
                    unit_b(b, j, 2)
                    route_b(b, j, 7)
                    unit_a(b, j, 3)
                    route_b(b, j, 8)
                    unit_b(b, j, 3)
                    route_b(b, j, 9)
                q_lo(b, j)
                x_stats(b, j)
                if behind:
                    route_b(b, j, 10)
                    unit_a(b, j, 4)
                    route_b(b, j, 11)
                    unit_b(b, j, 4)
                    route_b(b, j, 12)
                    unit_a(b, j, 5)
                    route_b(b, j, 13)
                    unit_b(b, j, 5)
                def between(i):
                    if behind and i < 3:
                        route_b(b, j, 14 + i)
                    if behind and i == 2 and j < 2:
                        last_lo(b, j)

                if behind and j >= 2:
                    last_lo(b, j)
                attended(b, j, 1, between)
                if s in turns if isinstance(s, int) else False:
                    for n in turns[s]:
                        split(n)

            def block_table():
                link, c = chained(dve, "tab_steps", 0, 0)
                dve.wait_ge(sem("count_done"), 1)
                cnt, nb, cb_, base_ = tc[:, 0, :], tc[:, 1, :], tc[:, 2, :], tc[:, 3, :]
                dve.wait_ge(sem("xz_done"), NP + 1)
                link(dve.tensor_copy(cnt, s_banks[0][:, 0:NE]))
                link(ts(tc[:, 4, :], cnt, float(P - 1), None, ALU.add))
                link(dve.tensor_copy(tci[:, :], tc[:, 4, :]))
                link(ts(tci[:, :], tci[:, :], 7, None, ALU.logical_shift_right))
                link(dve.tensor_copy(nb, tci[:, :]))
                src = nb
                for i, step_ in enumerate((1, 2, 4)):
                    dst = tc[:, 5 + i, :]
                    dve.tensor_copy(dst[:, 0:step_], src[:, 0:step_])
                    link(tt(dst[:, step_:NE], src[:, step_:NE], src[:, 0:NE - step_], ALU.add))
                    src = dst
                link(tt(tc[:, 8, :], cnt, eoff[:, 0, :], ALU.add))
                dve.tensor_copy(pad_i[0:1, :], tc[0:1, 8, :]).then_inc(sem("pad_ready"), 1)
                link(ts(tc[:, 9, :], nb, -float(P), float(ROWS), ALU.mult, ALU.add))
                blk_b = blk[0:1, :].rearrange("p (n o) -> p n o", o=1).to_broadcast([1, NBLK, NE])
                ends_b = src[0:1, :].rearrange("p (o e) -> p o e", o=1).to_broadcast([1, NBLK, NE])
                gain_b = tc[0:1, 9, :].rearrange("p (o e) -> p o e", o=1).to_broadcast([1, NBLK, NE])
                link(tt(tb[:, :, :], blk_b, ends_b, ALU.is_ge))
                link(dve.tensor_reduce(tw[:, 0, :], tb[:, :, 0:NE - 1], AX.X, ALU.add))
                link(tt(tbb[:, :, :], tb[:, :, :], gain_b, ALU.mult))
                link(dve.tensor_reduce(tw[:, 1, :], tbb[:, :, 0:NE - 1], AX.X, ALU.add))
                link(ts(tc[:, 10, :], src, -float(P), float(NE * ROWS), ALU.mult, ALU.add))
                link(stt(tw[:, 2, :], tw[:, 1, :], tc[0:1, 10, NE - 1:NE], tb[:, :, NE - 1], ALU.subtract, ALU.mult))
                link(tt(tw[:, 1, :], tw[:, 1, :], tw[:, 2, :], ALU.subtract))
                link(stt(tw[:, 1, :], blk[:, :], float(P), tw[:, 1, :], ALU.mult, ALU.add))
                dve.tensor_copy(tab_e[:, :], tw[:, 0, :])
                dve.tensor_copy(tab_r[:, :], tw[:, 1, :]).then_inc(sem("table_done"), 1)

            def final_slot():
                y_norm(B, 0)
                route_c(B, 0)
                v_lo(B, -1)
                w2_turn(0, 3)
                y_rows(B, 0)
                shared_sum(B, 0, 0)
                shared_sum(B, 0, 1)
                route_a(B, 0)
                unit_a(B, 0, 0)
                route_b(B, 0, 0, 1, 2, 3)
                unit_b(B, 0, 0)
                route_b(B, 0, 4, 5, 6, 7)
                unit_a(B, 0, 1)
                route_b(B, 0, 8, 9, 10, 11)
                unit_b(B, 0, 1)
                route_b(B, 0, 12, 13, 14, 15, 16)
                unit_a(B, 0, 2)
                unit_b(B, 0, 2)
                w2_turn(3, 4)
                unit_a(B, 0, 3)
                unit_b(B, 0, 3)
                block_table()
                route_c(B, 1)
                unit_a(B, 0, 4)
                unit_b(B, 0, 4)
                unit_a(B, 0, 5)
                unit_b(B, 0, 5)
                w2_turn(4, 5)
                last_lo(B, 0)
                w2_turn(5, NE)
                shared_sum(B, 1, 0)
                shared_sum(B, 1, 1)

            dve.memset(half[:, :], -0.5)
            dve.memset(ones[:, :], 1.0)
            dve.memset(cum[:, :, :, :], 0.0).then_inc(sem("dconst_done"), 1)
            x_stats(0, -2)
            dve.wait_ge(sem("gam_loaded"), 32)
            dve.tensor_copy(gam[:, 0, :], gam_in[:, 0, :])
            dve.tensor_copy(gam[:, 1, :], gam_in[:, 1, :])
            dve.tensor_copy(wR[:, :, 0, :], r_in[:, :, :]).then_inc(sem("gam_done"), 1)
            dve.wait_ge(sem("gam_done"), 1)
            tt(wR[:, :, 1, :], r_in[:, :, :], wR[:, :, 0, :].bitcast(f32), ALU.subtract)
            x_norm(0, -1)
            x_stats(0, -1)
            dve.wait_ge(sem("consts_built"), 3)
            dve.tensor_copy(ident16[:, :], identf[:, :])
            dve.tensor_copy(identr[:, :], identf[:, :])
            dve.tensor_copy(mask[:, :, :], maskf[:, :, :])
            dve.tensor_copy(upper[:, :], upf[:, :]).then_inc(sem("consts_done"), 1)
            for n in range(2):
                dve.wait_ge(sem("wprod_hi"), n + 1)
                w = (wA, wV)[n]
                flat = lambda hl: w[:, hl, :, :].rearrange("p k n -> p (k n)")
                tt(flat(1), banks[n][:, :], flat(0).bitcast(f32), ALU.subtract).then_inc(sem("wprod_split"), 1)
            q_lo(0, -1)
            dve.wait_ge(sem("tables_built"), 1)
            slots(dve, slot)
            final_slot()

            def step(n, u):
                known = isinstance(n, int)
                if not known or 0 <= n < NBLK:
                    wait(dve, "eth_done", n + 1)
                    g = banks[2 + u % 2]
                    wait(dve, "ehT_tp", n - 1)
                    stt(eth[:, u % 2, :], eth[:, u % 2, :], 1.0, g[:, 0:FE], ALU.add, ALU.mult
                        ).then_inc(sem("ea_done"), 1)
                    wait(dve, "ea_done", n + 1)
                    stt(eh[:, u % 2, :], eth[:, u % 2, :], 0.5, g[:, FE:2 * FE], ALU.mult, ALU.mult
                        ).then_inc(sem("eh_done"), 1)
                if not known or 0 <= n - 1 < NBLK:
                    v = (u - 1) % 2
                    wait(dve, "ehThi_done", n)
                    flat = lambda hl: ehT[0:FH, v, hl, :, :].rearrange("p k n -> p (k n)")
                    tt(flat(1), banks[4 + v][0:FH, 0:256], flat(0).bitcast(f32), ALU.subtract
                       ).then_inc(sem("ehT_done"), 1)
                if not known or 0 <= n - 2 < NBLK:
                    r = (u - 2) % RING
                    wait(dve, "edown_done", n - 1)
                    if known:
                        wait(dve, f"scattered{r}", ((n - 2) // RING) * 16)
                    else:
                        dve.wait_ge(sem(f"scattered{r}"), (n - 2 - r) * 2)
                    dve.tensor_copy(eo[:, r, :], banks[6 + r % 2][:, 0:D]).then_inc(sem("eo_done"), 1)

            dve.wait_ge(sem("xs_done"), 2 * NP)
            for par in (0, 1):
                dve.wait_ge(sem(f"xs_stored{par}"), 16 * (NP // 2))
            for n in range(RING):
                step(n, n)
            with dve.Fori(1, NBLK // RING - 1) as i:
                for u in range(RING):
                    step(i * RING + u, u)
            for n in range(NBLK - RING, NBLK + 2):
                step(n, n % RING)

            def combine(pair, u, i):
                dve.wait_ge(sem(f"parts_loaded{u}"), i * 32 + 32)
                for k in range(2):
                    for t in range(2):
                        row = acc[:, ds(pair, 1), t, :].rearrange("p a d -> p (a d)")
                        w = wts[:, ds(pair, 1), k, t:t + 1].rearrange("p a t -> p (a t)")
                        ins = stt(row, cx[:, u, k, t, :], w, row, ALU.mult, ALU.add)
                    ins.then_inc(sem("combine_half" if k == 0 else "combined"), 1)
                    if k == 0:
                        dve.wait_ge(sem("combine_half"), pair + 1)

            dve.wait_ge(sem("acc_loaded"), 16 * NP)
            with dve.Fori(0, NP // PARTS) as i:
                for u in range(PARTS):
                    combine(i * PARTS + u, u, i)

        @block.gpsimd
        def _(pool):
            def x_pow(b, j, k):
                q = b * SLOTS + j + k
                par = (j + k) % 2
                wait(pool, "xbase_done", q + 1)
                wait(pool, "xz_done", q - 1)
                pool.tensor_tensor(r1[:, par, :, :], b1[:, :, :],
                                   half[:, :].rearrange("p (a t) -> p a t", a=2), ALU.pow
                                   ).then_inc(sem("xroots_done"), 1)
                wait(pool, "xroots_done", q + 1)
                pool.tensor_tensor(ratio[:, par, :], b1[:, 1, :], r1[:, par, 1, :], ALU.mult
                                   ).then_inc(sem("xinv_done"), 1)
                wait(pool, "xinv_done", q + 1)
                pool.tensor_tensor(ratio[:, par, :], ratio[:, par, :], r1[:, par, 0, :], ALU.mult
                                   ).then_inc(sem("xpow_done"), 1)

            def x_lo(b, j):
                q = b * SLOTS + j + 1
                c = ((j + 1) % SLOTS) * 2 * P
                wait(pool, "xhi_done", q + 1)
                pool.tensor_tensor(xT[:, 1, :, c:c + 2 * P], xg[:, :, :], xT[:, 0, :, c:c + 2 * P].bitcast(f32),
                                   ALU.subtract).then_inc(sem("xlo_done"), 1)

            def y_pow(b, j):
                p = b * SLOTS + j - 1
                par = (j + 1) % 2
                wait(pool, "ybase_done", p + 1)
                pool.tensor_tensor(r2[:, par, :], b2[:, :], half[:, 0:2], ALU.pow).then_inc(sem("ypow_done"), 1)

            def y_lo(b, j):
                p = b * SLOTS + j - 1
                par = (j + 1) % 2
                wait(pool, "y16hi_done", p + 1)
                pool.tensor_tensor(y16[:, par, 0, :, D:2 * D], ny[:, :, :], y16[:, par, 0, :, 0:D], ALU.subtract
                                   ).then_inc(sem("y16lo_done"), 1)

            def h_lo(b, j, u):
                p = b * SLOTS + j - 1
                wait(pool, "hhi_done", UNITS * p + u + 1)
                pool.tensor_tensor(hT[:, 1, u, :], h32[:, u % 2, :], hT[:, 0, u, :].bitcast(f32),
                                   ALU.subtract).then_inc(sem("hlo_done"), 1)

            def scatter(b, j):
                p = b * SLOTS + j - 2
                par = j % 2
                wait(pool, "dest_done", p + 1)
                wait(pool, "rows_ready", p + 1)
                wait(pool, "idle_done", p)
                pool.tensor_tensor(idle[:, :], half[:, 0:2], half[:, 0:2], ALU.add).then_inc(sem("idle_done"), 1)
                for k in range(2):
                    for t in range(2):
                        pool.indirect_dma_start(
                            out=row_tab, out_offset=bass.IndirectOffsetOnAxis(ap=di[:, par, k, t:t + 1], axis=0),
                            in_=y16[:, par, k, t, :], in_offset=None
                        ).then_inc(sem(f"rows_stored{par}"), 16)

            def slot(b, j, last=False):
                s = b * SLOTS + j
                behind, behind2 = (not isinstance(s, int) or s >= n for n in (1, 2))
                if behind:
                    y_pow(b, j)
                    y_lo(b, j)
                if behind2:
                    scatter(b, j)
                if not last:
                    x_lo(b, j)
                if behind:
                    for u in range(UNITS - 2):
                        h_lo(b, j, u)
                if not last:
                    x_pow(b, j, 2)
                if behind:
                    h_lo(b, j, UNITS - 2)

            pool.memset(identf[:, :], 0.0)
            pool.memset(maskf[:, :, :], 0.0)
            pool.memset(upf[:, :], 1.0)
            pool.memset(idle[:, :], 0.0).then_inc(sem("pconst"), 1)
            pool.wait_ge(sem("pconst"), 1)
            pool.affine_select(out=identf[:, :], in_=identf[:, :], compare_op=ALU.not_equal, fill=1.0, base=0,
                               pattern=[[-1, P]], channel_multiplier=1).then_inc(sem("consts_built"), 1)
            for a in range(2):
                pool.affine_select(out=maskf[:, a, a * P:(a + 1) * P], in_=maskf[:, a, a * P:(a + 1) * P],
                                   compare_op=ALU.is_ge, fill=MASKED, base=0, pattern=[[-1, P]],
                                   channel_multiplier=1)
            pool.affine_select(out=upf[:, :], in_=upf[:, :], compare_op=ALU.is_gt, fill=0.0, base=0,
                               pattern=[[1, P]], channel_multiplier=-1).then_inc(sem("consts_built"), 2)
            pool.wait_ge(sem("dconst_done"), 1)
            x_pow(0, -1, 1)
            pool.iota(idtab[:, :, :, :], [[2 * P, NP], [T, 2], [P, 2]], base=0, channel_multiplier=1)
            pool.iota(w8[:, :, :], [[0, 2], [-1, NE]], base=NE, channel_multiplier=0,
                      allow_small_or_imprecise_dtypes=True)
            pool.iota(eoff[:, :, :], [[0, 2], [ROWS, NE]], base=0, channel_multiplier=0,
                      allow_small_or_imprecise_dtypes=True)
            pool.iota(blk[:, :], [[1, NBLK]], base=0, channel_multiplier=0, allow_small_or_imprecise_dtypes=True
                      ).then_inc(sem("tables_built"), 1)
            x_pow(0, -1, 2)
            x_lo(0, -1)
            pool.memset(pads, 0.0).then_inc(sem("pads_zeroed"), 1)
            for n in range(2):
                wait(pool, "pads_zeroed", 1)
                wait(pool, "pads_stored", 16 * n)
                pool.iota(y16[:, :, :, :, :].bitcast(i32)[:, :, :, :, D], [[4 * P, 2], [2 * P, 2], [P, 2]],
                          base=2 * T + n * NE * P, channel_multiplier=1).then_inc(sem("pads_built"), 1)
            slots(pool, slot)
            slot(B, 0, last=True)
            scatter(B, 1)

            def scatter_block(n, u):
                wait(pool, "eo_done", n + 1)
                wait(pool, "idle_done", n + NP)
                pool.tensor_tensor(idle[:, :], half[:, 0:2], half[:, 0:2], ALU.add).then_inc(sem("idle_done"), 1)
                pool.indirect_dma_start(
                    out=exp_tab,
                    out_offset=bass.IndirectOffsetOnAxis(ap=rows[:, u, :].bitcast(i32)[:, D:D + 1], axis=0),
                    in_=eo[:, u, :], in_offset=None).then_inc(sem(f"scattered{u}"), 16)

            for u in range(RING):
                scatter_block(u, u)
            with pool.Fori(1, NBLK // RING) as i:
                for u in range(RING):
                    scatter_block(i * RING + u, u)
            for u in range(RING):
                pool.wait_ge(sem(f"scattered{u}"), 16 * (NBLK // RING))


def kernel(**inputs):
    import numpy as np
    import concourse.bacc as bacc
    from concourse.bass_utils import run_bass_kernel_spmd

    a = {k.removeprefix("L0_"): np.asarray(v) for k, v in inputs.items()}
    flat = np.ascontiguousarray
    qkv = a["attn_qkv"]
    gu = a["ffn_shared_gate_up_w"].T
    order = np.concatenate([np.arange(o + u * P, min(o + (u + 1) * P, o + F))
                            for u in range(UNITS) for o in (0, F)])
    router = np.zeros((D, 10), np.float32)
    router[:, 0:NE] = a["ffn_gate_w"].T
    router[:, NE:NE + 1] = a["ffn_shared_gate_w"].T
    arrays = {
        "x": a["attn_x"].reshape(T, D), "wqT": flat(qkv[:, 0:D].T), "wkT": flat(qkv[:, D:2 * D].T),
        "wvT": flat(qkv[:, 2 * D:].T), "wo": a["attn_o_proj"], 
        "gamma_beta": flat(np.stack([a["attn_gamma"], a["attn_beta"]]).reshape(2, KD, P).transpose(2, 0, 1)),
        "router": router, "wgu": flat(gu[:, order]), "wsd": flat(a["ffn_shared_down_w"].T),
        "w13": flat(a["ffn_w13"].transpose(0, 2, 1)), "w2": flat(a["ffn_w2"].transpose(0, 2, 1)),
    }
    nc = bacc.Bacc("TRN2", target_bir_lowering=False, num_devices=1)
    args = [nc.dram_tensor(n, v.shape, mybir.dt.from_np(v.dtype), kind="ExternalInput").ap()
            for n, v in arrays.items()]
    out = nc.dram_tensor("out", (T, D), mybir.dt.float32, kind="ExternalOutput").ap()
    program(nc, *args, out)
    r = run_bass_kernel_spmd(nc, [arrays], core_ids=[0])
    return r.results[0]["out"].reshape(B, S, D)
```
